# Optimizing a Trainium2 kernel written in Bass

```python
import numpy as np
import jax
import jax.numpy as jnp

def _softmax(x, axis=-1):
    return jax.nn.softmax(x, axis=axis)

def _gelu(x):
    return jax.nn.gelu(x, approximate=True)

def _silu(x):
    return jax.nn.silu(x)

def _sigmoid(x):
    return jax.nn.sigmoid(x)

def _layernorm(x, axis=-1, eps=1e-05):
    m = jnp.mean(x, axis=axis, keepdims=True)
    v = jnp.var(x, axis=axis, keepdims=True)
    return (x - m) / jnp.sqrt(v + eps)

def _scatter_add(tgt, idx, src, axis=0):
    return tgt.at[idx].add(src)

def _segment_sum(src, seg, n):
    return jax.ops.segment_sum(src, seg, n)
kernel_name = 'mk_flamingo_gated_d1_seqx_r4_d4dccf'

def setup_inputs(seed: int=0):
    np.random.seed(seed)
    _w = jnp.asarray

    def _rec_inputs():
        import jax
        import jax.numpy as jnp
        _rk = jax.random.key(seed)
        x = 7.22e-05 + 1 * jax.random.normal(jax.random.fold_in(_rk, 1), (4, 512, 512), jnp.float32)
        _lenS = 512 - jax.random.randint(jax.random.fold_in(_rk, 7), (4,), 0, max(1, 512 // 4) + 1, jnp.int32)
        _lenS2 = 1601 - jax.random.randint(jax.random.fold_in(_rk, 8), (4,), 0, max(1, 1601 // 4) + 1, jnp.int32)
        _ctx_2048P = jax.random.normal(jax.random.fold_in(_rk, 11), (4, 16, 512), jnp.float32)
        _ctx_2048c = jax.random.dirichlet(jax.random.fold_in(_rk, 511), 0.3 * jnp.ones((16,), jnp.float32), (4, 1601))
        _ctx_2048t = jnp.einsum('bsk,bkd->bsd', _ctx_2048c, _ctx_2048P)
        _ctx_2048t = _ctx_2048t * jax.lax.rsqrt(jnp.mean(jnp.square(_ctx_2048t)) + 1e-12) * 0.953939
        ctx_2048 = 4.13588e-05 + 0.999923 * (_ctx_2048t + 0.3 * jax.random.normal(jax.random.fold_in(_rk, 611), (4, 1601, 512), jnp.float32))
        _g = jax.random.normal(jax.random.fold_in(_rk, 9001), (2, 1), jnp.float32)
        _g = jnp.sign(_g) * jnp.maximum(jnp.abs(_g), 1.0) + (_g == 0) * 1.0
        g_xattn = _g[0]
        g_ffn = _g[1]
        return (x, ctx_2048, g_xattn, g_ffn)
    x, ctx_2048, g_xattn, g_ffn = _rec_inputs()

    def _L0_xattn_setup():
        import math
        import jax, jax.numpy as jnp
        import numpy as np
        HEADS = 16
        MASKED_BIAS = -10000.0

        def _mha(q, k, v):
            B, Sq, D = q.shape
            Sk = k.shape[-2]
            hd = D // HEADS
            qh = q.reshape(B, Sq, HEADS, hd).transpose(0, 2, 1, 3)
            kh = k.reshape(B, Sk, HEADS, hd).transpose(0, 2, 1, 3)
            vh = v.reshape(B, Sk, HEADS, hd).transpose(0, 2, 1, 3)
            scores = jnp.einsum('bhqd,bhkd->bhqk', qh, kh) / math.sqrt(hd)
            qi = jnp.arange(Sq)[:, None] + (Sk - Sq)
            ki = jnp.arange(Sk)[None, :]
            causal = ki <= qi
            scores = jnp.where(causal[None, None], scores, jnp.asarray(MASKED_BIAS, scores.dtype))
            attn = jax.nn.softmax(scores, axis=-1)
            out = jnp.einsum('bhqk,bhkd->bhqd', attn, vh)
            return out.transpose(0, 2, 1, 3).reshape(B, Sq, D)
        key = jax.random.key(seed)
        kq, kk, kv = jax.random.split(key, 3)
        B, S, D = (4, 256, 512)
        q = jax.random.normal(kq, (B, S, D), dtype=jnp.float32)
        k = jax.random.normal(kk, (B, S, D), dtype=jnp.float32)
        v = jax.random.normal(kv, (B, S, D), dtype=jnp.float32)
        return {'q': q, 'k': k, 'v': v}
    _L0_xattn_all = _L0_xattn_setup()
    _L0_xattn_in = {k: v for k, v in _L0_xattn_all.items() if k in ()}
    del _L0_xattn_all

    def _L0_ffn_setup():
        import jax, jax.numpy as jnp
        import numpy as np

        def _sparsify_2to4(h):
            B, S, I = h.shape
            g = h.reshape(B, S, I // 4, 4)
            a = jnp.abs(g)
            _, idx = jax.lax.top_k(a, 2)
            pos = jnp.arange(4)
            mask = (pos == idx[..., 0:1]) | (pos == idx[..., 1:2])
            return (g * mask.astype(g.dtype)).reshape(B, S, I)
        key = jax.random.key(seed)
        k1, k2, k3, k4 = jax.random.split(key, 4)
        B, S, H, I = (4, 512, 512, 2048)
        x = jax.random.normal(k1, (B, S, H), dtype=jnp.float32)
        w_gate = jax.random.normal(k2, (H, I), dtype=jnp.float32) / np.sqrt(H)
        w_up = jax.random.normal(k3, (H, I), dtype=jnp.float32) / np.sqrt(H)
        w_down = jax.random.normal(k4, (I, H), dtype=jnp.float32) / np.sqrt(I)
        return {'x': x, 'w_gate': w_gate, 'w_up': w_up, 'w_down': w_down}
    _L0_ffn_all = _L0_ffn_setup()
    _L0_ffn_in = {k: v for k, v in _L0_ffn_all.items() if k in ('w_gate', 'w_up', 'w_down')}
    del _L0_ffn_all
    return {'x': x, 'ctx_2048': ctx_2048, 'g_xattn': g_xattn, 'g_ffn': g_ffn, 'L0_ffn_w_gate': _L0_ffn_in['w_gate'], 'L0_ffn_w_up': _L0_ffn_in['w_up'], 'L0_ffn_w_down': _L0_ffn_in['w_down']}

def reference(x, ctx_2048, g_xattn, g_ffn, L0_ffn_w_gate, L0_ffn_w_up, L0_ffn_w_down):
    import jax
    import jax.numpy as jnp

    def _L0_xattn_ref(q, k, v):
        import math
        import jax, jax.numpy as jnp
        import numpy as np
        HEADS = 16
        MASKED_BIAS = -10000.0

        def _mha(q, k, v):
            B, Sq, D = q.shape
            Sk = k.shape[-2]
            hd = D // HEADS
            qh = q.reshape(B, Sq, HEADS, hd).transpose(0, 2, 1, 3)
            kh = k.reshape(B, Sk, HEADS, hd).transpose(0, 2, 1, 3)
            vh = v.reshape(B, Sk, HEADS, hd).transpose(0, 2, 1, 3)
            scores = jnp.einsum('bhqd,bhkd->bhqk', qh, kh) / math.sqrt(hd)
            qi = jnp.arange(Sq)[:, None] + (Sk - Sq)
            ki = jnp.arange(Sk)[None, :]
            causal = ki <= qi
            scores = jnp.where(causal[None, None], scores, jnp.asarray(MASKED_BIAS, scores.dtype))
            attn = jax.nn.softmax(scores, axis=-1)
            out = jnp.einsum('bhqk,bhkd->bhqd', attn, vh)
            return out.transpose(0, 2, 1, 3).reshape(B, Sq, D)
        return _mha(q, k, v)

    def _L0_ffn_ref(x, w_gate, w_up, w_down):
        import jax, jax.numpy as jnp
        import numpy as np

        def _sparsify_2to4(h):
            B, S, I = h.shape
            g = h.reshape(B, S, I // 4, 4)
            a = jnp.abs(g)
            _, idx = jax.lax.top_k(a, 2)
            pos = jnp.arange(4)
            mask = (pos == idx[..., 0:1]) | (pos == idx[..., 1:2])
            return (g * mask.astype(g.dtype)).reshape(B, S, I)
        h = jax.nn.silu(jnp.einsum('bsh,hi->bsi', x, w_gate)) * jnp.einsum('bsh,hi->bsi', x, w_up)
        h_sparse = _sparsify_2to4(h)
        return jnp.einsum('bsi,ih->bsh', h_sparse, w_down)
    x = x + jnp.tanh(g_xattn[0]) * _L0_xattn_ref(_layernorm(x, axis=-1), ctx_2048, ctx_2048)
    x = x + jnp.tanh(g_ffn[0]) * _L0_ffn_ref(_layernorm(x, axis=-1), L0_ffn_w_gate, L0_ffn_w_up, L0_ffn_w_down)
    return x

_drawn_inputs = setup_inputs


def setup_inputs(seed=0):
    import zlib

    import numpy as np

    out = dict(_drawn_inputs(seed))
    spreads = {}
    factors = {}
    for name, (base, spread) in spreads.items():
        noise = np.random.default_rng([zlib.crc32(name.encode()), seed]).standard_normal(out[name].shape)
        drawn = base * np.exp(spread * noise) if base else spread * noise
        out[name] = jnp.asarray(drawn.astype(out[name].dtype))
    for name, factor in factors.items():
        out[name] = (out[name] * factor).astype(out[name].dtype)
    return out
```

```python
from contextlib import ExitStack

import concourse.bass as bass
from concourse import mybir

F32 = mybir.dt.float32
F32R = mybir.dt.float32r
BF16 = mybir.dt.bfloat16
F16 = mybir.dt.float16
U32 = mybir.dt.uint32
ALU = mybir.AluOpType
ACT = mybir.ActivationFunctionType
AX = mybir.AxisListType

P = 128
HEADS = 16
HD = 32
EPS = 1e-5
MASKED = -1e30
S_BANKS = 2
M_BANKS = 3
P_RING = 8


def gated_cross_attention_ffn(nc, x, ctx_kv, g_xattn, g_ffn, w_gate, w_up, w_down, out):
    B, SQ, D = x.shape
    SK = ctx_kv.shape[1]
    INNER = w_gate.shape[1]
    QT = SQ // P
    HG = P // HD
    G = D // P
    UNITS = B * G
    KT = -(-SK // P)
    KLAST = SK - (KT - 1) * P
    SHIFT = SK - SQ
    SKP = SK + SK % 2
    SCALE = float(HD) ** -0.5
    VW = HD + 1

    def q_start(kt):
        return max(0, (P * kt - SHIFT) // 2 * 2)

    def key_rows(kt):
        return KLAST if kt == KT - 1 else P

    MASKW = P + 2

    def diagonal(kt):
        c0 = P * kt - SHIFT
        if c0 + P <= 0:
            return None
        if c0 < 0:
            return 1 - c0, MASKW - (1 - c0)
        return 0, min(MASKW, SQ - q_start(kt))

    def max_chunks(t):
        end = SHIFT + P * t + P + 1
        end += end % 2
        cuts = list(range(0, end, 512)) + [end]
        if cuts[-2] > end - P:
            cuts[-2] = end - P
        return [(a, b - a) for a, b in zip(cuts, cuts[1:])]

    CHUNKS = [(t, a, w) for t in range(QT) for a, w in max_chunks(t)]
    NCH = len(CHUNKS)
    PER_T = [len(max_chunks(t)) for t in range(QT)]
    EXPS = 2 * KT
    GROUPS = -(-KT // 4)
    TG = GROUPS + 1
    STACK_DMAS = 2 * 3 * 2
    SCAN = G * INNER // 8

    x_v = x.rearrange("b (t p) (g d) -> p b g t d", p=P, g=G)
    ctx_v = ctx_kv.rearrange("b s (g d) -> b g s d", g=G)
    out_v = out.rearrange("b (t p) d -> b t p d", p=P)

    with ExitStack() as outer:
        def sem(name):
            return outer.enter_context(nc.semaphore(name))

        def keep(name, shape, dt=F32):
            return outer.enter_context(nc.sbuf_tensor(name, shape, dt))

        x_sb = keep("x_sb", [P, UNITS, QT, P])
        ident = keep("ident", [P, P])
        gates = keep("gates", [P, 2])
        tanhs = keep("tanhs", [P, 2])
        stats = keep("stats", [P, B * QT, 6])
        mv = keep("mv", [P, B * QT, 2])
        var = keep("var", [P, B * QT])
        root = keep("root", [P, B * QT])
        rstd = keep("rstd", [P, B * QT])
        tmp_s = keep("tmp_s", [P, B * QT])
        w_raw = keep("w_raw", [P, 3, SCAN])
        inv_scale = keep("inv_scale", [P, 3])
        w_scale = keep("w_scale", [P, 3])
        w_loaded = [sem(f"w_loaded{i}") for i in range(3)]
        ln_chain = sem("ln_chain")
        root_ready = sem("root_ready")
        gates_loaded = sem("gates_loaded")
        tanh_ready = sem("tanh_ready")
        x_loaded = [sem("x_loaded_first"), sem("x_loaded_rest")]
        sp_passed = sem("sp_passed")
        pool_passed = sem("pool_passed")

        def norm_stats(dve, turn, b0, b1):
            done = [turn * 8]
            n0, n1 = QT * b0, QT * b1
            s = slice(n0, n1)

            def link(ins):
                ins.then_inc(ln_chain, 1)
                done[0] += 1
                dve.wait_ge(ln_chain, done[0])

            for n in range(n0, n1):
                last = dve.bn_stats(stats[:, n, :], x_sb[:, G * (n // QT):G * (n // QT) + G, n % QT, :])
            link(last)
            for n in range(n0, n1):
                last = dve.bn_aggr(mv[:, n, :], stats[:, n, :])
            link(last)
            link(dve.tensor_scalar(var[:, s], mv[:, s, 1], EPS, None, ALU.add))
            dve.wait_ge(root_ready, turn + 1)
            link(dve.reciprocal(rstd[:, s], root[:, s]))
            link(dve.tensor_tensor(tmp_s[:, s], rstd[:, s], rstd[:, s], ALU.mult))
            link(dve.scalar_tensor_tensor(tmp_s[:, s], tmp_s[:, s], -0.5, var[:, s], ALU.mult, ALU.mult))
            link(dve.scalar_tensor_tensor(root[:, s], tmp_s[:, s], 1.5, rstd[:, s], ALU.add, ALU.mult))
            link(dve.tensor_copy(rstd[:, s], root[:, s]))

        def norm_root(act, turn, b0, b1):
            act.wait_ge(ln_chain, 8 * turn + 3)
            act.activation(root[:, QT * b0:QT * b1], var[:, QT * b0:QT * b1], ACT.Sqrt).then_inc(root_ready, 1)

        JB = INNER // SQ
        M = 4
        PIECES = 6 * JB
        w_rest = sem("w_rest")

        def load_piece(sp, q):
            j, kind, half = q // 6, q % 6 // 2, q % 2
            if q >= 3:
                sp.wait_ge(w_rest, q - 2)
            dst = w_raw[:, q % 3, :].rearrange("p (a n) -> p a n", a=2)
            if kind < 2:
                w = (w_gate, w_up)[kind].rearrange("(c p) n -> p c n", p=P)
                src = w[:, 2 * half:2 * half + 2, SQ * j:SQ * j + SQ]
            else:
                src = w_down[SQ * j:SQ * j + SQ, :].rearrange("(p m) d -> p m d", m=M)[:, 2 * half:2 * half + 2, :]
            sp.dma_start(dst, src).then_inc(w_loaded[q % 3], 16)

        with ExitStack() as ctx:
            def sb(name, shape, dt=F32):
                return ctx.enter_context(nc.sbuf_tensor(name, shape, dt))

            def pb(name, shape, dt=F32):
                return ctx.enter_context(nc.psum_tensor(name, shape, dt))

            kv_sb = sb("kv_sb", [P, 2, KT, P])
            v_ones = sb("v_ones", [P, 2, KT, HG, VW + 1])
            kT_hi = sb("kT_hi", [P, SKP], F32R)
            kT_lo = sb("kT_lo", [P, SKP], F32R)
            qT_hi = sb("qT_hi", [P, SQ], F32R)
            qT_lo = sb("qT_lo", [P, SQ], F32R)
            k_stack = sb("k_stack", [3 * HD + 1, 4 * 2, SKP], F32R)
            q_stack = sb("q_stack", [3 * HD + 1, 4 * 2, SQ], F32R)
            xq = sb("xq", [P, 2, QT, P])
            probs = sb("probs", [P, P_RING, SQ])
            oT = sb("oT", [64 + VW, 2, SQ])
            ident_b = sb("ident_b", [P, P], BF16)
            mask_k = sb("mask_k", [P, MASKW], BF16)
            mask_q = sb("mask_q", [P, P], BF16)
            mean_u = sb("mean_u", [P, UNITS, QT])
            rstd_u = sb("rstd_u", [P, UNITS, QT])
            max_part = sb("max_part", [P, 2, 2, NCH])
            neg_max = sb("neg_max", [P, 2, 2, QT], BF16)
            den_inv = sb("den_inv", [P, QT, 2])
            att = sb("att", [P, QT, 2, HD])
            amax_part = sb("amax_part", [P, 3, 8])
            amax = sb("amax", [P, 3])
            amax_all = sb("amax_all", [P, 3])
            pow2 = sb("pow2", [P, 3])

            ps_max = [pb(f"ps_max{i}", [P, 512]) for i in range(M_BANKS)]
            ps_s = [pb(f"ps_s{i}", [P, 512]) for i in range(S_BANKS)]
            ps_o = pb("ps_o", [P, 512])
            ps_t = pb("ps_t", [P, 512])
            ps_m = pb("ps_m", [P, 512])

            consts_zero = sem("consts_zero")
            consts_ready = sem("consts_ready")
            ones_row = sem("ones_row")
            kv_loaded = [sem("kv_loaded0"), sem("kv_loaded1")]
            v_ready = sem("v_ready")
            unit_stats = sem("unit_stats")
            xq_ready = sem("xq_ready")
            t_ready = sem("t_ready")
            hi_ready = sem("hi_ready")
            lo_ready = sem("lo_ready")
            stack_loaded = [sem(f"stack_loaded{i}") for i in range(4)]
            scan_loaded = sem("scan_loaded")
            scan_read = sem("scan_read")
            amax_ready = sem("amax_ready")
            amax_shared = sem("amax_shared")
            scale_chain = sem("scale_chain")
            max_scored = sem("max_scored")
            max_read = sem("max_read")
            neg_ready = sem("neg_ready")
            row_ready = sem("row_ready")
            row_copied = sem("row_copied")
            s_ready = sem("s_ready")
            exp_done = sem("exp_done")
            pv_done = sem("pv_done")
            o_copied = sem("o_copied")
            ot_ready = sem("ot_ready")
            tail_chain = sem("tail_chain")
            x_added = sem("x_added")

            block = ctx.enter_context(nc.Block())

            LOOPS = UNITS // 2 - 1

            def all_periods(eng, period):
                period(0, 0, True, 2)
                with eng.Fori(0, LOOPS) as it:
                    for c in range(1, 4):
                        period(it, c, True, 2)
                    period(it + 1, 0, True, 2)
                for c in range(1, 4):
                    period(LOOPS, c, False, 3 - c)

            def chunks_at(p, c, kt, left):
                if isinstance(p, int) and p == 0:
                    return [(1 + i // (2 * NCH), 1 + i // (2 * NCH), i % (2 * NCH)) for i in range(4 * kt, 4 * kt + 4)]
                return [(p + 2, (c + 2) % 4, i) for i in (2 * kt, 2 * kt + 1)] if left == 2 else []

            def max_reads_before(p, i):
                n = 2 * NCH
                last = i - M_BANKS if i >= M_BANKS else (n - 1 - (n - 1 - i) % M_BANKS) - n
                return n * p + last + 1 + M_BANKS

            TURN_STEPS = {0: {8: 0, 10: 1, 12: 2}, 1: {1: 3, 3: 4}}

            def join_step(p):
                return 7 if isinstance(p, int) and p == 0 else 0

            def row_steps(p):
                return (9, 10) if isinstance(p, int) and p == 0 else (4, 5)

            @block.sync
            def _(sp):
                for i, g in enumerate((g_xattn, g_ffn)):
                    sp.dma_start(gates[:, i:i + 1], g.rearrange("(a n) -> a n", a=1).partition_broadcast(P)
                                 ).then_inc(gates_loaded, 16)

                def load_kv(b, g, par):
                    src = ctx_v[b, g]
                    sp.dma_start(kv_sb[:, par, 0:KT - 1, :],
                                 src[0:(KT - 1) * P, :].rearrange("(t p) d -> p t d", p=P)
                                 ).then_inc(kv_loaded[par], 16)
                    sp.dma_start(kv_sb[0:KLAST, par, KT - 1, :], src[(KT - 1) * P:SK, :]
                                 ).then_inc(kv_loaded[par], 16)

                def load_x(b):
                    for g in range(G):
                        sp.dma_start(x_sb[:, b * G + g, :, :], x_v[:, b, g]).then_inc(x_loaded[min(b, 1)], 16)

                def scan_weights(n):
                    if not (isinstance(n, int) and n == 0):
                        sp.wait_ge(scan_read, n)
                        sp.sem_inc(sp_passed, 1)
                    for i, w in enumerate((w_gate, w_up, w_down)):
                        src = w.rearrange("a n -> (a n)").rearrange("(p n k) -> n p k", p=P, k=SCAN)
                        sp.dma_start(w_raw[:, i, :], src[n]).then_inc(scan_loaded, 16)

                def fill_stacks(v, par, r):
                    if not (isinstance(v, int) and v < 2):
                        sp.wait_ge(s_ready, EXPS * (2 * (v - 2) + r + 1))
                    for done, stack, parts in ((TG - 1, k_stack, (kT_hi, kT_hi, kT_lo)),
                                               (TG, q_stack, (qT_hi, qT_lo, qT_hi))):
                        sp.wait_ge(lo_ready, TG * v + done)
                        for j in (2 * r, 2 * r + 1):
                            for n, part in enumerate(parts):
                                sp.dma_start(stack[HD * n:HD * n + HD, 4 * par + j, :].bitcast(F32),
                                             part[HD * j:HD * j + HD, :].bitcast(F32)
                                             ).then_inc(stack_loaded[2 * par + r], 16)

                def free_kv(v):
                    sp.wait_ge(t_ready, TG * v + GROUPS)
                    sp.sem_inc(sp_passed, 1)
                    sp.wait_ge(v_ready, 2 * (v + 1))
                    sp.sem_inc(sp_passed, 1)

                load_kv(0, 0, 0)
                load_x(0)
                load_kv(0, 1, 1)
                fill_stacks(0, 0, 0)
                fill_stacks(0, 0, 1)
                for b in range(1, B):
                    load_x(b)
                free_kv(0)
                load_kv(0, 2, 0)
                fill_stacks(1, 1, 0)

                def period(it, c, more, left):
                    par, r = c // 2, c % 2
                    u = 2 * it + par
                    if r == 0 and (more or c == 0):
                        fill_stacks(u + 1, 1 - par, 1)
                    if c == 0:
                        scan_weights(it)
                    if r == 1 and more:
                        free_kv(u + 1)
                        if c == 1:
                            load_kv((it + 1) // 2, 2 * ((it + 1) % 2) + 1, 1)
                        else:
                            load_kv(((it + 2) // 2) % B, 2 * ((it + 2) % 2), 0)
                        fill_stacks(u + 2, par, 0)

                all_periods(sp, period)
                sp.wait_ge(scan_read, 8)
                for q in range(3):
                    load_piece(sp, q)
                sp.wait_ge(kv_loaded[0], 32 * (UNITS // 2 + 1))

            @block.gpsimd
            def _(pool):
                pool.memset(ident[:, :], 0.0)
                pool.memset(ident_b[:, :], 0.0)
                pool.memset(mask_k[:, :], 0.0)
                pool.memset(mask_q[:, :], 0.0)
                pool.memset(v_ones[:, :, :, :, :], 1.0)
                pool.memset(kT_hi[:, SK:SKP].bitcast(F32), 0.0)
                pool.memset(kT_lo[:, SK:SKP].bitcast(F32), 0.0)
                pool.memset(oT[:, :, :], 0.0).then_inc(consts_zero, 1)
                pool.wait_ge(consts_zero, 1)
                for m in (ident, ident_b):
                    pool.affine_select(out=m[:, :], in_=m[:, :], compare_op=ALU.not_equal, fill=1.0,
                                       base=0, pattern=[[-1, P]], channel_multiplier=1)
                pool.affine_select(out=mask_k[:, :], in_=mask_k[:, :], compare_op=ALU.is_gt, fill=MASKED,
                                   base=0, pattern=[[1, MASKW]], channel_multiplier=-1)
                pool.affine_select(out=mask_q[:, :], in_=mask_q[:, :], compare_op=ALU.is_gt, fill=MASKED,
                                   base=0, pattern=[[-1, P]], channel_multiplier=1).then_inc(consts_ready, 1)

                def copy_v(v, loads, par):
                    pool.wait_ge(kv_loaded[par], 32 * loads)
                    if not (isinstance(v, int) and v < 2):
                        pool.wait_ge(pv_done, 2 * EXPS * (v - 1) + P_RING)
                    pool.sem_inc(pool_passed, 1)
                    pool.tensor_copy(v_ones[:, par, 0:KT - 1, :, 0:HD],
                                     kv_sb[:, par, 0:KT - 1, :].rearrange("p t (h d) -> p t h d", h=HG)
                                     ).then_inc(v_ready, 1)
                    pool.tensor_copy(v_ones[0:KLAST, par, KT - 1, :, 0:HD],
                                     kv_sb[0:KLAST, par, KT - 1, :].rearrange("p (h d) -> p h d", h=HG)
                                     ).then_inc(v_ready, 1)

                copy_v(0, 1, 0)

                def period(it, c, more, left):
                    par = c // 2
                    if c == 0 or (c == 2 and more):
                        copy_v(2 * it + par + 1, it + 1 + par, 1 - par)

                all_periods(pool, period)
                pool.wait_ge(amax_ready, 1)
                pool.partition_all_reduce(amax_all[:, :], amax[:, :], P, bass.bass_isa.ReduceOp.max
                                          ).then_inc(amax_shared, 1)

            @block.scalar
            def _(act):
                act.sem_inc(exp_done, S_BANKS)
                act.sem_inc(o_copied, 1)
                norm_root(act, 0, 0, 1)
                act.wait_ge(gates_loaded, 32)
                act.activation(tanhs[:, :], gates[:, :], ACT.Tanh).then_inc(tanh_ready, 1)

                def round_hi(v, i):
                    act.wait_ge(t_ready, TG * v + i + 1)
                    if i < GROUPS:
                        w = min(512, SK - 512 * i)
                        act.activation(kT_hi[:, 512 * i:512 * i + w], ps_t[:, 0:w], ACT.Copy).then_inc(hi_ready, 1)
                    else:
                        act.activation(qT_hi[:, :], ps_t[:, :], ACT.Copy).then_inc(hi_ready, 1)

                def copy_row(p, c, hh):
                    act.wait_ge(row_ready, 2 * p + hh + 1)
                    act.activation(q_stack[3 * HD:3 * HD + 1, 2 * c + hh, :], ps_m[3 * HD:3 * HD + 1, :],
                                   ACT.Copy).then_inc(row_copied, 1)

                def copy_o(p, c):
                    act.wait_ge(pv_done, EXPS * (p + 1) + P_RING)
                    act.wait_ge(ot_ready, p + 1)
                    act.activation(oT[:, c % 2, :], ps_o[0:64 + VW, :], ACT.Copy).then_inc(o_copied, 1)

                for i in range(TG):
                    round_hi(0, i)
                for hh in range(2):
                    copy_row(0, 0, hh)
                for i in (0, 1):
                    act.wait_ge(stack_loaded[i], 16 * STACK_DMAS)
                for i in range(TG):
                    round_hi(1, i)
                norm_root(act, 1, 1, B)

                def period(it, c, more, left):
                    p = 4 * it + c
                    u = 2 * it + c // 2
                    if c == 2 and not more:
                        norm_root(act, 2, 0, B - 1)
                    for kt in range(KT):
                        K, w = key_rows(kt), SQ - q_start(kt)
                        for hh in range(2):
                            e = 2 * kt + hh
                            act.wait_ge(s_ready, EXPS * p + e + 1)
                            act.wait_ge(pv_done, EXPS * p + e + 1)
                            act.activation(probs[0:K, (EXPS * c + e) % P_RING, 0:w], ps_s[hh][0:K, 0:w],
                                           ACT.Exp, scale=SCALE).then_inc(exp_done, 1)
                        if kt == 0:
                            if not (isinstance(p, int) and p == 0):
                                copy_o(p - 1, (c + 3) % 4)
                        if more and kt in TURN_STEPS[c % 2]:
                            if TURN_STEPS[c % 2][kt] == 0:
                                for r in range(2):
                                    act.wait_ge(stack_loaded[2 * (1 - c // 2) + r],
                                                16 * STACK_DMAS * (it + 1 + c // 2))
                            round_hi(u + 2, TURN_STEPS[c % 2][kt])
                        if left and kt in row_steps(p):
                            copy_row(p + 1, (c + 1) % 4, row_steps(p).index(kt))

                all_periods(act, period)
                copy_o(4 * LOOPS + 3, 3)

            @block.vector
            def _(dve):
                dve.sem_inc(max_read, M_BANKS)
                dve.memset(ps_o[:, :], 0.0)
                dve.memset(k_stack[3 * HD:3 * HD + 1, :, :].bitcast(F32), 1.0).then_inc(ones_row, 1)

                def unit_norms(turn, b0, b1):
                    for dst, src in ((mean_u, mv[:, :, 0]), (rstd_u, rstd[:, :])):
                        dve.tensor_copy(
                            dst[:, :, :].rearrange("p (b g) t -> p b g t", b=B)[:, b0:b1],
                            src.rearrange("p (b t) -> p b t", b=B)[:, b0:b1].unsqueeze(2).to_broadcast(
                                [P, b1 - b0, G, QT])).then_inc(unit_stats, 1)
                    dve.wait_ge(unit_stats, 2 * (turn + 1))

                dve.wait_ge(x_loaded[0], 16 * G)
                norm_stats(dve, 0, 0, 1)
                unit_norms(0, 0, 1)

                def norm_q(u, par):
                    for t in range(QT):
                        last = dve.tensor_scalar(xq[:, par, t, :], x_sb[:, u, t, :], mean_u[:, u, t:t + 1],
                                                 rstd_u[:, u, t:t + 1], ALU.subtract, ALU.mult)
                    last.then_inc(xq_ready, 1)

                def rest_lo(v, i):
                    dve.wait_ge(hi_ready, TG * v + i + 1)
                    if i < GROUPS:
                        s = slice(512 * i, min(SK, 512 * i + 512))
                        dve.tensor_tensor(kT_lo[:, s], ps_t[:, 0:s.stop - s.start], kT_hi[:, s].bitcast(F32),
                                          ALU.subtract).then_inc(lo_ready, 1)
                    else:
                        dve.tensor_tensor(qT_lo[:, :], ps_t[:, :], qT_hi[:, :].bitcast(F32),
                                          ALU.subtract).then_inc(lo_ready, 1)

                def read_max(p, c, i):
                    hh, n = i // NCH, i % NCH
                    dve.wait_ge(max_scored, 2 * NCH * p + i + 1)
                    dve.tensor_reduce(max_part[:, c % 2, hh, n:n + 1], ps_max[i % M_BANKS][:, 0:CHUNKS[n][2]],
                                      AX.X, ALU.max).then_inc(max_read, 1)

                def join_max(p, c):
                    dve.wait_ge(max_read, 2 * NCH * (p + 1) + M_BANKS)
                    n, t = PER_T[0], PER_T.index(PER_T[-1])
                    dve.tensor_reduce(neg_max[:, c % 2, :, 0:t],
                                      max_part[:, c % 2, :, 0:n * t].rearrange("p h (t n) -> p h t n", n=n),
                                      AX.X, ALU.max, negate=True).then_inc(neg_ready, 1)
                    dve.tensor_reduce(neg_max[:, c % 2, :, t:QT],
                                      max_part[:, c % 2, :, n * t:NCH].rearrange("p h (t n) -> p h t n", t=QT - t),
                                      AX.X, ALU.max, negate=True).then_inc(neg_ready, 1)

                def add_attention(p, c, u):
                    o = ps_m[:, :].rearrange("p (t w) -> p t w", t=QT)
                    dve.wait_ge(ot_ready, p + 3)
                    dve.reciprocal(den_inv[:, :, :], o[:, :, HD:HD + 65:64]).then_inc(tail_chain, 1)
                    dve.wait_ge(tail_chain, 2 * p + 1)
                    for hh in range(2):
                        last = dve.scalar_tensor_tensor(
                            att[:, :, hh, :], o[:, :, 64 * hh:64 * hh + HD], tanhs[:, 0:1],
                            den_inv[:, :, hh:hh + 1].to_broadcast([P, QT, HD]), ALU.mult, ALU.mult)
                    last.then_inc(tail_chain, 1)
                    dve.wait_ge(tail_chain, 2 * p + 2)
                    xs = x_sb[:, u, :, 64 * (c % 2):64 * (c % 2) + 64]
                    dve.tensor_tensor(xs, xs, att[:, :, :, :].rearrange("p t h d -> p t (h d)"),
                                      ALU.add).then_inc(x_added, 1)

                norm_q(0, 0)
                for i in range(TG):
                    rest_lo(0, i)
                for i in range(2 * NCH):
                    read_max(0, 0, i)
                join_max(0, 0)
                norm_q(1, 1)
                for i in range(TG):
                    rest_lo(1, i)
                dve.wait_ge(x_loaded[1], 16 * G * (B - 1))
                norm_stats(dve, 1, 1, B)
                unit_norms(1, 1, B)
                dve.wait_ge(tanh_ready, 1)

                def read_scan(n):
                    dve.wait_ge(scan_loaded, 48 * (n + 1))
                    dve.tensor_reduce(amax_part[:, :, n], w_raw[:, :, :], AX.X, ALU.max,
                                      apply_absolute_value=True).then_inc(scan_read, 1)

                def join_scans():
                    dve.wait_ge(scan_read, 8)
                    dve.tensor_reduce(amax[:, :], amax_part[:, :, :], AX.X, ALU.max).then_inc(amax_ready, 1)

                def weight_scales():
                    dve.wait_ge(amax_shared, 1)
                    dve.tensor_scalar(amax[:, :], amax_all[:, :], 1e-30, None, ALU.max).then_inc(scale_chain, 1)
                    dve.wait_ge(scale_chain, 1)
                    dve.tensor_scalar(pow2[:, :].bitcast(U32), amax[:, :].bitcast(U32), 0x7F800000, None,
                                      ALU.bitwise_and).then_inc(scale_chain, 1)
                    dve.wait_ge(scale_chain, 2)
                    dve.tensor_scalar(inv_scale[:, :], pow2[:, :], 2.0 ** -14, None, ALU.mult
                                      ).then_inc(scale_chain, 1)
                    dve.wait_ge(scale_chain, 3)
                    dve.reciprocal(w_scale[:, :], inv_scale[:, :]).then_inc(scale_chain, 1)

                def period(it, c, more, left):
                    p = 4 * it + c
                    u = 2 * it + c // 2
                    if c % 2 == 1 and more:
                        norm_q(u + 2, c // 2)
                    if c == 1 and not more:
                        join_scans()
                    if c == 2 and not more:
                        weight_scales()
                        norm_stats(dve, 2, 0, B - 1)
                    for kt in range(KT):
                        if left and kt == join_step(p):
                            join_max(p + 1, (c + 1) % 4)
                        for chunk in chunks_at(p, c, kt, left):
                            read_max(*chunk)
                        if kt == 2:
                            prev = 2 * it - 1 if c == 0 else 2 * it + (c - 1) // 2
                            if not (isinstance(p, int) and p == 0):
                                add_attention(p - 1, (c + 3) % 4, prev)
                        if more and kt in TURN_STEPS[c % 2]:
                            rest_lo(u + 2, TURN_STEPS[c % 2][kt])
                        if c == 0 and kt == 8:
                            read_scan(it)

                all_periods(dve, period)
                add_attention(4 * LOOPS + 3, 3, 2 * LOOPS + 1)

            @block.tensor
            def _(pe):
                pe.sem_inc(pv_done, P_RING)
                pe.sem_inc(ot_ready, 2)
                pe.wait_ge(consts_ready, 1)
                pe.wait_ge(ones_row, 1)

                def turn(v, loads, par, i):
                    pe.wait_ge(lo_ready, TG * v + i)
                    if i < GROUPS:
                        pe.wait_ge(kv_loaded[par], 32 * loads)
                        for t in range(4 * i, min(KT, 4 * i + 4)):
                            K = key_rows(t)
                            last = pe.transpose(ps_t[:, P * (t % 4):P * (t % 4) + K], kv_sb[0:K, par, t, :],
                                                ident[0:K, 0:K])
                    else:
                        pe.wait_ge(xq_ready, v + 1)
                        for t in range(QT):
                            last = pe.transpose(ps_t[:, P * t:P * t + P], xq[:, par, t, :], ident[:, :])
                    last.then_inc(t_ready, 1)

                def score_max(p, c, i):
                    hh, n = i // NCH, i % NCH
                    t, a, w = CHUNKS[n]
                    bank = ps_max[i % M_BANKS]
                    pe.wait_ge(max_read, max_reads_before(p, i))
                    masked = n + 1 == NCH or CHUNKS[n + 1][0] != t
                    last = pe.matmul(bank[:, 0:w], q_stack[0:3 * HD, 2 * c + hh, P * t:P * t + P],
                                     k_stack[0:3 * HD, 2 * c + hh, a:a + w], start=True, stop=True)
                    if masked:
                        last = pe.matmul(bank[:, w - P:w], ident_b[:, :], mask_q[:, :], start=False, stop=True,
                                         skip_group_check=True)
                    last.then_inc(max_scored, 1)

                def max_row(p, c, hh):
                    pe.wait_ge(neg_ready, 2 * (p + 1))
                    for t in range(QT):
                        last = pe.matmul(ps_m[3 * HD:3 * HD + 1, P * t:P * t + P], neg_max[:, c % 2, hh, t:t + 1],
                                         ident_b[:, :], start=True, stop=True)
                    last.then_inc(row_ready, 1)

                def score(p, c, kt, hh):
                    K, q0, slot = key_rows(kt), q_start(kt), 2 * c + hh
                    pe.wait_ge(exp_done, EXPS * p + 2 * kt + hh + 1)
                    d = diagonal(kt)
                    last = pe.matmul(ps_s[hh][0:K, 0:SQ - q0], k_stack[:, slot, P * kt:P * kt + K],
                                     q_stack[:, slot, q0:SQ], start=True, stop=True)
                    if d:
                        m0, w = d
                        last = pe.matmul(ps_s[hh][0:K, 0:w], ident_b[0:K, 0:K], mask_k[0:K, m0:m0 + w],
                                         start=False, stop=True, skip_group_check=True)
                    last.then_inc(s_ready, 1)

                def values(p, c, kt, hh, unit=None):
                    K, q0, e = key_rows(kt), q_start(kt), 2 * kt + hh
                    pe.wait_ge(exp_done, EXPS * p + e + 1 + S_BANKS)
                    if kt == 0 and hh == 0:
                        pe.wait_ge(o_copied, p + 1)
                        pe.wait_ge(v_ready, 2 * unit + 2)
                    pe.matmul(ps_o[64 * hh:64 * hh + VW, q0:SQ],
                              v_ones[0:K, c // 2, kt, 2 * (c % 2) + hh, 0:VW],
                              probs[0:K, (EXPS * c + e) % P_RING, 0:SQ - q0],
                              start=kt == 0, stop=kt == KT - 1, skip_group_check=True).then_inc(pv_done, 1)

                def turn_o(p, c):
                    pe.wait_ge(o_copied, p + 2)
                    for t in range(QT):
                        last = pe.transpose(ps_m[:, P * t:P * t + 64 + VW], oT[:, c % 2, P * t:P * t + P],
                                            ident[0:64 + VW, 0:64 + VW])
                    last.then_inc(ot_ready, 1)

                for i in range(TG):
                    turn(0, 1, 0, i)
                pe.wait_ge(stack_loaded[0], 16 * STACK_DMAS)
                for i in range(2 * NCH):
                    score_max(0, 0, i)
                max_row(0, 0, 0)
                pe.wait_ge(row_copied, 1)
                max_row(0, 0, 1)
                for i in range(TG):
                    turn(1, 1, 1, i)

                def period(it, c, more, left):
                    p = 4 * it + c
                    u = 2 * it + c // 2
                    first = isinstance(p, int) and p == 0
                    if left == 2:
                        if first:
                            pe.wait_ge(stack_loaded[1], 16 * STACK_DMAS)
                        else:
                            pe.wait_ge(stack_loaded[(c + 2) % 4], 16 * STACK_DMAS * (it + 1 + c // 2))
                    for kt in range(KT):
                        chunks = chunks_at(p, c, kt, left)
                        half = len(chunks) // 2
                        if kt == 0:
                            pe.wait_ge(row_copied, 2 * (p + 1))
                        score(p, c, kt, 0)
                        for chunk in chunks[:half]:
                            if first and chunk[0] == 2 and chunk[2] == 0:
                                pe.wait_ge(stack_loaded[2], 16 * STACK_DMAS)
                            score_max(*chunk)
                        score(p, c, kt, 1)
                        if more and kt in TURN_STEPS[c % 2]:
                            turn(u + 2, it + 2, c // 2, TURN_STEPS[c % 2][kt])
                        if kt == 2 and not first:
                            turn_o(p - 1, (c + 3) % 4)
                        if left and kt == row_steps(p)[0]:
                            if not first:
                                pe.wait_ge(x_added, p)
                            max_row(p + 1, (c + 1) % 4, 0)
                        if left and kt == row_steps(p)[1]:
                            pe.wait_ge(row_copied, 2 * (p + 1) + 1)
                            max_row(p + 1, (c + 1) % 4, 1)
                        for hh in range(2):
                            if kt > 0:
                                values(p, c, kt - 1, hh, u)
                            elif not first:
                                values(p - 1, (c + 3) % 4, KT - 1, hh)
                        for chunk in chunks[half:]:
                            if first and chunk[0] == 2 and chunk[2] == 0:
                                pe.wait_ge(stack_loaded[2], 16 * STACK_DMAS)
                            score_max(*chunk)

                all_periods(pe, period)
                p = 4 * LOOPS + 3
                for hh in range(2):
                    values(p, 3, KT - 1, hh)
                pe.wait_ge(x_added, p)
                turn_o(p, 3)

        with ExitStack() as ctx:
            def sb(name, shape, dt=F32):
                return ctx.enter_context(nc.sbuf_tensor(name, shape, dt))

            def pb(name, shape, dt=F32):
                return ctx.enter_context(nc.psum_tensor(name, shape, dt))

            IT = JB * M
            X_SCALE = 256.0
            HID_SCALE = 2.0 ** -50

            wg_hi, wg_lo, wu_hi, wu_lo = (sb(n, [P, G, INNER], F16) for n in ("wg_hi", "wg_lo", "wu_hi", "wu_lo"))
            wd_hi, wd_lo = (sb(n, [P, JB, M, D], F16) for n in ("wd_hi", "wd_lo"))
            xn = sb("xn", [P, QT, G, P])
            xT_hi = sb("xT_hi", [P, G, SQ], F16)
            xT_lo = sb("xT_lo", [P, G, SQ], F16)
            silu = sb("silu", [P, 2, SQ])
            hid = sb("hid", [P, 2, SQ])
            mag = sb("mag", [P, M, SQ])
            hid_hi = sb("hid_hi", [P, M, SQ], F16)
            hid_lo = sb("hid_lo", [P, M, SQ], F16)
            beats = sb("beats", [P, 6, SQ], F16)
            wins = sb("wins", [P, M, SQ], F16)
            kept_hi = sb("kept_hi", [P, M, SQ], F16)
            kept_lo = sb("kept_lo", [P, M, SQ], F16)
            tanh_scale = sb("tanh_scale", [P, 1])
            out_scale = sb("out_scale", [P, 1])

            ps_g = [pb(f"ps_g{i}", [P, 512]) for i in range(2)]
            ps_u = [pb(f"ps_u{i}", [P, 512]) for i in range(2)]
            ps_d = [pb(f"ps_d{i}", [P, 512]) for i in range(QT)]

            w_round = sem("w_round")
            factors = sem("factors")
            xn_ready = sem("xn_ready")
            xt_turned = sem("xt_turned")
            xt_hi_ready = sem("xt_hi_ready")
            xt_lo_ready = sem("xt_lo_ready")
            gate_ready = sem("gate_ready")
            up_ready = sem("up_ready")
            tanh_done = sem("tanh_done")
            silu_ready = sem("silu_ready")
            hid_ready = sem("hid_ready")
            mag_ready = sem("mag_ready")
            hid_hi_ready = sem("hid_hi_ready")
            hid_lo_ready = sem("hid_lo_ready")
            beats_ready = sem("beats_ready")
            wins_ready = sem("wins_ready")
            kept_ready = sem("kept_ready")
            down_ready = sem("down_ready")
            kept_used = sem("kept_used")
            y_ready = sem("y_ready")
            y_stored = sem("y_stored")

            block = ctx.enter_context(nc.Block())

            def weights_of(q):
                j, kind, half = q // 6, q % 6 // 2, q % 2
                if kind < 2:
                    hi, lo = ((wg_hi, wg_lo), (wu_hi, wu_lo))[kind]
                    return kind, *(w[:, 2 * half:2 * half + 2, SQ * j:SQ * j + SQ] for w in (hi, lo))
                return kind, *(w[:, j, 2 * half:2 * half + 2, :] for w in (wd_hi, wd_lo))

            def raw(q):
                return w_raw[:, q % 3, :].rearrange("p (a n) -> p a n", a=2)

            def pieces_after(i):
                j, m = i // M, i % M
                return range(6 * (j + 1) + 2 * m, 6 * (j + 1) + 2 * m + 2) if m < 3 and j + 1 < JB else ()

            def all_batches(eng, batch):
                batch(0, True)
                with eng.Fori(1, B) as b:
                    batch(b, False)

            @block.sync
            def _(sp):
                for q in range(3, PIECES):
                    load_piece(sp, q)

                def store(b):
                    for t in range(QT):
                        sp.wait_ge(y_ready, QT * b + t + 1)
                        sp.sem_inc(sp_passed, 1)
                        xv = x_sb[:, :, t, :].rearrange("p (b g) d -> p b g d", b=B)
                        sp.dma_start(out_v[b, t].rearrange("p (g d) -> p g d", g=G), xv[:, b]).then_inc(y_stored, 16)

                with sp.Fori(0, B) as b:
                    store(b)
                sp.wait_ge(y_stored, 16 * B * QT)

            @block.scalar
            def _(act):
                def split(q):
                    kind, hi, _lo = weights_of(q)
                    act.wait_ge(w_loaded[q % 3], 16 * (q // 3 + 1))
                    act.activation(hi, raw(q), ACT.Copy, scale=w_scale[:, kind:kind + 1]).then_inc(w_round, 1)

                def batch(b, first):
                    for c in range(G):
                        act.wait_ge(xt_turned, G * b + c + 1)
                        if c == 0 and not first:
                            act.wait_ge(up_ready, IT * b)
                        act.activation(xT_hi[:, c, :], ps_g[c % 2][:, :], ACT.Copy, scale=X_SCALE
                                       ).then_inc(xt_hi_ready, 1)
                    if first:
                        split(3)
                        act.wait_ge(factors, 2)
                    for i in range(IT):
                        n = IT * b + i
                        s = i % 2
                        act.wait_ge(gate_ready, n + 1)
                        if not (first and i < 2):
                            act.wait_ge(hid_ready, n - 1)
                        act.activation(silu[:, s, :], ps_g[s][:, :], ACT.Tanh, scale=tanh_scale[:, 0:1]
                                       ).then_inc(tanh_done, 1)
                        if first and i == 0:
                            for q in (4, 5):
                                split(q)
                        act.wait_ge(hid_ready, n + 1)
                        if i % M == 0 and not (first and i == 0):
                            act.wait_ge(kept_ready, JB * b + i // M)
                        act.activation(mag[:, i % M, :], hid[:, s, :], ACT.Abs).then_inc(mag_ready, 1)
                        act.activation(hid_hi[:, i % M, :], hid[:, s, :], ACT.Copy).then_inc(hid_hi_ready, 1)
                        if first:
                            for q in pieces_after(i):
                                split(q)

                for q in range(3):
                    split(q)
                norm_root(act, 3, B - 1, B)
                all_batches(act, batch)

            @block.vector
            def _(dve):
                def norm_tokens(b):
                    if not isinstance(b, int):
                        dve.wait_ge(xt_turned, G * b)
                    for t in range(QT):
                        last = dve.tensor_scalar(xn[:, t, :, :],
                                                 x_sb[:, :, t, :].rearrange("p (b g) d -> p b g d", b=B)[:, b],
                                                 mv[:, :, 0].rearrange("p (b t) -> p b t", b=B)[:, b, t:t + 1],
                                                 rstd[:, :].rearrange("p (b t) -> p b t", b=B)[:, b, t:t + 1],
                                                 ALU.subtract, ALU.mult)
                    last.then_inc(xn_ready, 1)

                def split(q):
                    kind, hi, lo = weights_of(q)
                    dve.wait_ge(w_round, q + 1)
                    dve.scalar_tensor_tensor(lo, raw(q), w_scale[:, kind:kind + 1], hi, ALU.mult, ALU.subtract
                                             ).then_inc(w_rest, 1)

                def select(k):
                    dve.wait_ge(mag_ready, M * (k + 1))
                    dve.tensor_tensor(beats[:, 0:3, :], mag[:, 0:3, :], mag[:, 1:4, :], ALU.is_ge)
                    dve.tensor_tensor(beats[:, 3:5, :], mag[:, 0:2, :], mag[:, 2:4, :], ALU.is_ge)
                    dve.tensor_tensor(beats[:, 5, :], mag[:, 0, :], mag[:, 3, :], ALU.is_ge
                                      ).then_inc(beats_ready, 1)
                    dve.wait_ge(beats_ready, k + 1)
                    dve.tensor_tensor(wins[:, 0:2, :], beats[:, 0:2, :], beats[:, 3:5, :], ALU.add)
                    dve.tensor_tensor(wins[:, 2, :], beats[:, 2, :], beats[:, 3, :], ALU.subtract)
                    dve.tensor_tensor(wins[:, 3, :], beats[:, 2, :], beats[:, 4, :], ALU.add
                                      ).then_inc(wins_ready, 1)
                    dve.wait_ge(wins_ready, 3 * k + 1)
                    dve.tensor_tensor(wins[:, 1:3, :], wins[:, 1:3, :], beats[:, 0:2, :], ALU.subtract)
                    dve.tensor_tensor(wins[:, 0, :], wins[:, 0, :], beats[:, 5, :], ALU.add)
                    dve.tensor_tensor(wins[:, 3, :], wins[:, 3, :], beats[:, 5, :], ALU.add
                                      ).then_inc(wins_ready, 1)
                    dve.wait_ge(wins_ready, 3 * k + 2)
                    for m, (least, op) in enumerate(((1.5, ALU.is_gt), (0.5, ALU.is_gt), (-0.5, ALU.is_gt),
                                                     (1.5, ALU.is_lt))):
                        last = dve.tensor_scalar(wins[:, m, :], wins[:, m, :], least, None, op)
                    last.then_inc(wins_ready, 1)
                    dve.wait_ge(wins_ready, 3 * k + 3)
                    dve.wait_ge(hid_lo_ready, M * (k + 1))
                    if not (isinstance(k, int) and k == 0):
                        dve.wait_ge(kept_used, k)
                    dve.tensor_tensor(kept_hi[:, :, :], hid_hi[:, :, :], wins[:, :, :], ALU.mult)
                    dve.tensor_tensor(kept_lo[:, :, :], hid_lo[:, :, :], wins[:, :, :], ALU.mult
                                      ).then_inc(kept_ready, 1)

                def add_down(b):
                    for t in range(QT):
                        dve.wait_ge(down_ready, QT * b + t + 1)
                        xv = x_sb[:, :, t, :].rearrange("p (b g) d -> p b g d", b=B)[:, b]
                        dve.scalar_tensor_tensor(xv, ps_d[t][:, :].rearrange("p (g d) -> p g d", g=G),
                                                 out_scale[:, 0:1], xv, ALU.mult, ALU.add).then_inc(y_ready, 1)

                def batch(b, first):
                    if not first:
                        norm_tokens(b)
                        select(JB * b - 1)
                    for c in range(G):
                        dve.wait_ge(xt_hi_ready, G * b + c + 1)
                        dve.scalar_tensor_tensor(xT_lo[:, c, :], ps_g[c % 2][:, :], X_SCALE, xT_hi[:, c, :],
                                                 ALU.mult, ALU.subtract).then_inc(xt_lo_ready, 1)
                    if first:
                        for q in range(4):
                            split(q)
                    for i in range(IT):
                        n = IT * b + i
                        s = i % 2
                        dve.wait_ge(tanh_done, n + 1)
                        dve.scalar_tensor_tensor(silu[:, s, :], silu[:, s, :], 1.0, ps_g[s][:, :],
                                                 ALU.add, ALU.mult).then_inc(silu_ready, 1)
                        dve.wait_ge(silu_ready, n + 1)
                        dve.wait_ge(up_ready, n + 1)
                        if not (first and i < 2):
                            dve.wait_ge(hid_lo_ready, n - 1)
                        dve.scalar_tensor_tensor(hid[:, s, :], silu[:, s, :], HID_SCALE, ps_u[s][:, :],
                                                 ALU.mult, ALU.mult).then_inc(hid_ready, 1)
                        if first and i == 0:
                            for q in (4, 5):
                                split(q)
                        dve.wait_ge(hid_hi_ready, n + 1)
                        dve.tensor_tensor(hid_lo[:, i % M, :], hid[:, s, :], hid_hi[:, i % M, :],
                                          ALU.subtract).then_inc(hid_lo_ready, 1)
                        if first:
                            for q in pieces_after(i):
                                split(q)
                        if i % M == M - 1 and i < IT - 1:
                            select(JB * b + i // M)
                        if i == M and not first:
                            add_down(b - 1)

                norm_tokens(0)
                norm_stats(dve, 3, B - 1, B)
                dve.tensor_scalar(tanh_scale[:, :], inv_scale[:, 0:1], 0.5 / X_SCALE, None, ALU.mult
                                  ).then_inc(factors, 1)
                dve.tensor_scalar(out_scale[:, :], inv_scale[:, 0:1], inv_scale[:, 1:2],
                                  0.5 / (X_SCALE * X_SCALE * HID_SCALE), ALU.mult, ALU.mult).then_inc(factors, 1)
                dve.wait_ge(factors, 2)
                dve.tensor_scalar(out_scale[:, :], out_scale[:, :], inv_scale[:, 2:3], tanhs[:, 1:2],
                                  ALU.mult, ALU.mult).then_inc(factors, 1)
                all_batches(dve, batch)
                select(JB * B - 1)
                dve.wait_ge(factors, 3)
                add_down(B - 1)

            @block.tensor
            def _(pe):
                def down(b, j):
                    k = JB * b + j
                    pe.wait_ge(kept_ready, k + 1)
                    if j == 0 and not (isinstance(b, int) and b == 0):
                        pe.wait_ge(y_ready, QT * b)
                    for t in range(QT):
                        rows = slice(P * t, P * t + P)
                        for m in range(M):
                            for n, (a, w) in enumerate(((kept_hi, wd_hi), (kept_hi, wd_lo), (kept_lo, wd_hi))):
                                last = pe.matmul(ps_d[t][:, :], a[:, m, rows], w[:, j, m, :],
                                                 start=(j == 0 and m == 0 and n == 0),
                                                 stop=(j == JB - 1 and m == M - 1 and n == 2))
                        if j == JB - 1:
                            last.then_inc(down_ready, 1)
                        elif t == QT - 1:
                            last.then_inc(kept_used, 1)
                    if j == JB - 1:
                        pe.sem_inc(kept_used, 1)

                def batch(b, first):
                    pe.wait_ge(xn_ready, b + 1)
                    for c in range(G):
                        if c < 2:
                            if not first:
                                pe.wait_ge(silu_ready, IT * b)
                        else:
                            pe.wait_ge(xt_lo_ready, G * b + c - 1)
                        for t in range(QT):
                            last = pe.transpose(ps_g[c % 2][:, P * t:P * t + P], xn[:, t, c, :], ident[:, :])
                        last.then_inc(xt_turned, 1)
                    if not first:
                        down(b - 1, JB - 1)
                    pe.wait_ge(xt_lo_ready, G * (b + 1))
                    for i in range(IT):
                        j, m = i // M, i % M
                        n = IT * b + i
                        s = i % 2
                        if first and m == 0:
                            pe.wait_ge(w_rest, 6 * j + 4)
                        for w_hi, w_lo, bank, read, ready in ((wg_hi, wg_lo, ps_g[s], silu_ready, gate_ready),
                                                              (wu_hi, wu_lo, ps_u[s], hid_ready, up_ready)):
                            if not (first and i < 2):
                                pe.wait_ge(read, n - 1)
                            cols = slice(SQ * j + m, SQ * j + SQ, M)
                            for c in range(G):
                                for k, (w, xx) in enumerate(((w_hi, xT_hi), (w_hi, xT_lo), (w_lo, xT_hi))):
                                    last = pe.matmul(bank[:, :], w[:, c, cols], xx[:, c, :],
                                                     start=c == 0 and k == 0, stop=c == G - 1 and k == 2)
                            last.then_inc(ready, 1)
                        if m == M - 1 and j > 0:
                            if first:
                                pe.wait_ge(w_rest, 6 * j)
                            down(b, j - 1)

                all_batches(pe, batch)
                down(B - 1, JB - 1)


_INS = ["x", "ctx_2048", "g_xattn", "g_ffn", "L0_ffn_w_gate", "L0_ffn_w_up", "L0_ffn_w_down"]


def kernel(**inputs):
    import numpy as _np
    import concourse.bacc as _bacc
    from concourse import mybir as _mybir
    from concourse.bass_utils import run_bass_kernel_spmd as _run

    nc = _bacc.Bacc("TRN2", target_bir_lowering=False, num_devices=1)
    arrays, args = {}, []
    for name in _INS:
        a = _np.ascontiguousarray(inputs[name])
        arrays[f"in_{name}_dram"] = a
        args.append(nc.dram_tensor(f"in_{name}_dram", a.shape, _mybir.dt.from_np(a.dtype), kind="ExternalInput").ap())
    shape = _np.asarray(inputs["x"]).shape
    y = nc.dram_tensor("out_0_dram", shape, _mybir.dt.float32, kind="ExternalOutput").ap()
    gated_cross_attention_ffn(nc, *args, y)
    r = _run(nc, [arrays], core_ids=[0])
    return r.results[0]["out_0_dram"]
```

```python
from contextlib import ExitStack

import concourse.bass as bass
from concourse import mybir

F32 = mybir.dt.float32
F32R = mybir.dt.float32r
BF16 = mybir.dt.bfloat16
F16 = mybir.dt.float16
U32 = mybir.dt.uint32
ALU = mybir.AluOpType
ACT = mybir.ActivationFunctionType
AX = mybir.AxisListType

P = 128
HEADS = 16
HD = 32
EPS = 1e-5
MASKED = -1e30
S_BANKS = 2
M_BANKS = 3
P_RING = 8


def gated_cross_attention_ffn(nc, x, ctx_kv, g_xattn, g_ffn, w_gate, w_up, w_down, out):
    B, SQ, D = x.shape
    SK = ctx_kv.shape[1]
    INNER = w_gate.shape[1]
    QT = SQ // P
    HG = P // HD
    G = D // P
    UNITS = B * G
    KT = -(-SK // P)
    KLAST = SK - (KT - 1) * P
    SHIFT = SK - SQ
    SKP = SK + SK % 2
    SCALE = float(HD) ** -0.5
    VW = HD + 1

    def q_start(kt):
        return max(0, (P * kt - SHIFT) // 2 * 2)

    def key_rows(kt):
        return KLAST if kt == KT - 1 else P

    MASKW = P + 2

    def diagonal(kt):
        c0 = P * kt - SHIFT
        if c0 + P <= 0:
            return None
        if c0 < 0:
            return 1 - c0, MASKW - (1 - c0)
        return 0, min(MASKW, SQ - q_start(kt))

    def max_chunks(t):
        end = SHIFT + P * t + P + 1
        end += end % 2
        cuts = list(range(0, end, 512)) + [end]
        if cuts[-2] > end - P:
            cuts[-2] = end - P
        return [(a, b - a) for a, b in zip(cuts, cuts[1:])]

    CHUNKS = [(t, a, w) for t in range(QT) for a, w in max_chunks(t)]
    NCH = len(CHUNKS)
    PER_T = [len(max_chunks(t)) for t in range(QT)]
    EXPS = 2 * KT
    GROUPS = -(-KT // 4)
    TG = GROUPS + 1
    STACK_DMAS = 2 * 3 * 2
    SCAN = G * INNER // 8

    x_v = x.rearrange("b (t p) (g d) -> p b g t d", p=P, g=G)
    ctx_v = ctx_kv.rearrange("b s (g d) -> b g s d", g=G)
    out_v = out.rearrange("b (t p) d -> b t p d", p=P)

    with ExitStack() as outer:
        def sem(name):
            return outer.enter_context(nc.semaphore(name))

        def keep(name, shape, dt=F32):
            return outer.enter_context(nc.sbuf_tensor(name, shape, dt))

        x_sb = keep("x_sb", [P, UNITS, QT, P])
        ident = keep("ident", [P, P])
        gates = keep("gates", [P, 2])
        tanhs = keep("tanhs", [P, 2])
        stats = keep("stats", [P, QT, 6])
        mv = keep("mv", [P, QT, 2])
        var = keep("var", [P, QT])
        root = keep("root", [P, QT])
        tmp_s = keep("tmp_s", [P, QT])
        mean = keep("mean", [P, B, QT])
        rstd = keep("rstd", [P, B, QT])
        w_raw = keep("w_raw", [P, 3, SCAN])
        inv_scale = keep("inv_scale", [P, 3])
        w_scale = keep("w_scale", [P, 3])
        w_loaded = [sem(f"w_loaded{i}") for i in range(3)]
        ln_chain = sem("ln_chain")
        rstd_ready = sem("rstd_ready")
        gates_loaded = sem("gates_loaded")
        tanh_ready = sem("tanh_ready")
        x_loaded = [sem("x_loaded_first"), sem("x_loaded_rest")]
        sp_passed = sem("sp_passed")
        pool_passed = sem("pool_passed")
        dve_passed = sem("dve_passed")

        NORM_PARTS = QT + 4
        NORM_LINKS = [0] * QT + [1, 6, 9, 12, 14]

        def norm_part(dve, turn, b, i):
            done = [NORM_LINKS[-1] * turn + NORM_LINKS[i]]
            v, y, t = (w[:, :] for w in (var, root, tmp_s))

            def link(ins):
                ins.then_inc(ln_chain, 1)
                done[0] += 1
                dve.wait_ge(ln_chain, done[0])

            if i < QT:
                xs = x_sb[:, :, i, :].rearrange("p (b g) d -> p b g d", b=B)[:, b]
                last = dve.bn_stats(stats[:, i, :], xs)
                if i == QT - 1:
                    link(last)
                    dve.sem_inc(dve_passed, 1)
            elif i == QT:
                for n in range(QT):
                    last = dve.bn_aggr(mv[:, n, :], stats[:, n, :])
                link(last)
                dve.tensor_copy(mean[:, b, :], mv[:, :, 0])
                link(dve.tensor_scalar(v, mv[:, :, 1], EPS, None, ALU.add))
                link(dve.reciprocal(t, v))
                link(dve.tensor_scalar(t.bitcast(U32), t.bitcast(U32), 1, None, ALU.logical_shift_right))
                link(dve.tensor_scalar(y, t, 0.97 * 2.0 ** 63.5, None, ALU.mult))
            else:
                link(dve.tensor_tensor(t, y, y, ALU.mult))
                link(dve.scalar_tensor_tensor(t, t, -0.5, v, ALU.mult, ALU.mult))
                if i < NORM_PARTS - 1:
                    link(dve.scalar_tensor_tensor(y, t, 1.5, y, ALU.add, ALU.mult))
                else:
                    dve.scalar_tensor_tensor(rstd[:, b, :], t, 1.5, y, ALU.add, ALU.mult).then_inc(rstd_ready, 1)

        JB = INNER // SQ
        M = 4
        PIECES = 6 * JB

        ORDER = [(0, 0), (0, 1), *((j - k // 2, k) for j in range(1, JB) for k in range(3)), (JB - 1, 2)]
        w_rest = sem("w_rest")

        def load_piece(sp, q):
            j, kind, half = *ORDER[q // 2], q % 2
            if q >= 3:
                sp.wait_ge(w_rest, q - 2)
            dst = w_raw[:, q % 3, :].rearrange("p (a n) -> p a n", a=2)
            if kind < 2:
                w = (w_gate, w_up)[kind].rearrange("(c p) n -> p c n", p=P)
                src = w[:, 2 * half:2 * half + 2, SQ * j:SQ * j + SQ]
            else:
                src = w_down[SQ * j:SQ * j + SQ, :].rearrange("(p m) d -> p m d", m=M)[:, 2 * half:2 * half + 2, :]
            sp.dma_start(dst, src).then_inc(w_loaded[q % 3], 16)

        with ExitStack() as ctx:
            def sb(name, shape, dt=F32):
                return ctx.enter_context(nc.sbuf_tensor(name, shape, dt))

            def pb(name, shape, dt=F32):
                return ctx.enter_context(nc.psum_tensor(name, shape, dt))

            kv_sb = sb("kv_sb", [P, 2, KT, P])
            v_ones = sb("v_ones", [P, 2, KT, HG, VW + 1])
            kT_hi = sb("kT_hi", [P, SKP], F32R)
            kT_lo = sb("kT_lo", [P, SKP], F32R)
            qT_hi = sb("qT_hi", [P, SQ], F32R)
            qT_lo = sb("qT_lo", [P, SQ], F32R)
            k_stack = sb("k_stack", [3 * HD + 1, 4 * 2, SKP], F32R)
            q_stack = sb("q_stack", [3 * HD + 1, 4 * 2, SQ], F32R)
            xq = sb("xq", [P, 2, QT, P])
            probs = sb("probs", [P, P_RING, SQ])
            oT = sb("oT", [64 + VW, 2, SQ])
            ident_b = sb("ident_b", [P, P], BF16)
            mask_k = sb("mask_k", [P, MASKW], BF16)
            mask_q = sb("mask_q", [P, P], BF16)
            mean_u = sb("mean_u", [P, UNITS, QT])
            rstd_u = sb("rstd_u", [P, UNITS, QT])
            max_part = sb("max_part", [P, 2, 2, NCH])
            neg_max = sb("neg_max", [P, 2, 2, QT], BF16)
            den_inv = sb("den_inv", [P, QT, 2])
            att = sb("att", [P, QT, 2, HD])
            amax_part = sb("amax_part", [P, 3, 8, 1])
            amax = sb("amax", [P, 3])
            amax_all = sb("amax_all", [P, 3])
            pow2 = sb("pow2", [P, 3])

            ps_max = [pb(f"ps_max{i}", [P, 512]) for i in range(M_BANKS)]
            ps_s = [pb(f"ps_s{i}", [P, 512]) for i in range(S_BANKS)]
            ps_o = pb("ps_o", [P, 512])
            ps_t = pb("ps_t", [P, 512])
            ps_m = pb("ps_m", [P, 512])

            consts_zero = sem("consts_zero")
            consts_ready = sem("consts_ready")
            ones_row = sem("ones_row")
            kv_loaded = [sem("kv_loaded0"), sem("kv_loaded1")]
            v_ready = sem("v_ready")
            unit_stats = sem("unit_stats")
            xq_ready = sem("xq_ready")
            t_ready = sem("t_ready")
            hi_ready = sem("hi_ready")
            lo_ready = sem("lo_ready")
            stack_loaded = [sem(f"stack_loaded{i}") for i in range(4)]
            scan_loaded = sem("scan_loaded")
            scan_read = sem("scan_read")
            amax_ready = sem("amax_ready")
            amax_shared = sem("amax_shared")
            scale_chain = sem("scale_chain")
            max_scored = sem("max_scored")
            max_read = sem("max_read")
            neg_ready = sem("neg_ready")
            row_ready = sem("row_ready")
            row_copied = sem("row_copied")
            s_ready = sem("s_ready")
            exp_done = sem("exp_done")
            pv_done = sem("pv_done")
            o_copied = sem("o_copied")
            ot_ready = sem("ot_ready")
            tail_chain = sem("tail_chain")
            x_added = sem("x_added")

            block = ctx.enter_context(nc.Block())

            LOOPS = UNITS // 2 - 1

            def all_periods(eng, period):
                period(0, 0, True, 2)
                with eng.Fori(0, LOOPS) as it:
                    for c in range(1, 4):
                        period(it, c, True, 2)
                    period(it + 1, 0, True, 2)
                for c in range(1, 4):
                    period(LOOPS, c, False, 3 - c)

            CUTS = [0, 2, 4, 5, 8, 11, 14, 17, 19, 21, 23, 24, 25, 26]

            def chunks_at(p, c, kt, left):
                if isinstance(p, int) and p == 0:
                    return [(1 + i // (2 * NCH), 1 + i // (2 * NCH), i % (2 * NCH)) for i in range(4 * kt, 4 * kt + 4)]
                return [(p + 2, (c + 2) % 4, i) for i in range(CUTS[kt], CUTS[kt + 1])] if left == 2 else []

            def score_bank(kt, hh, left):
                return ps_s[hh] if left == 2 or (kt + left) % 2 == 1 else ps_max[hh]

            START_BANKS = [ps_t, ps_m, ps_s[0], ps_s[1], ps_t]
            START_CHUNKS = {14: 0, 17: 1, 20: 2, 22: 3, 24: 4}

            def turn_bank(v, i):
                return START_BANKS[i] if isinstance(v, int) and v < 2 else ps_t

            def max_reads_before(p, i):
                n = 2 * NCH
                last = i - M_BANKS if i >= M_BANKS else (n - 1 - (n - 1 - i) % M_BANKS) - n
                return n * p + last + 1 + M_BANKS

            TURN_STEPS = {0: {8: 0, 10: 1, 12: 2}, 1: {1: 3, 3: 4}}

            def join_step(p):
                return 7 if isinstance(p, int) and p == 0 else 0

            def row_steps(p):
                return (9, 10) if isinstance(p, int) and p == 0 else (4, 5)

            @block.sync
            def _(sp):
                for i, g in enumerate((g_xattn, g_ffn)):
                    sp.dma_start(gates[:, i:i + 1], g.rearrange("(a n) -> a n", a=1).partition_broadcast(P)
                                 ).then_inc(gates_loaded, 16)

                def load_kv(b, g, par):
                    src = ctx_v[b, g]
                    sp.dma_start(kv_sb[:, par, 0:KT - 1, :],
                                 src[0:(KT - 1) * P, :].rearrange("(t p) d -> p t d", p=P)
                                 ).then_inc(kv_loaded[par], 16)
                    sp.dma_start(kv_sb[0:KLAST, par, KT - 1, :], src[(KT - 1) * P:SK, :]
                                 ).then_inc(kv_loaded[par], 16)

                def load_x(b):
                    for g in range(G):
                        sp.dma_start(x_sb[:, b * G + g, :, :], x_v[:, b, g]).then_inc(x_loaded[min(b, 1)], 16)

                def scan_weights(n):
                    sp.wait_ge(scan_read, 3 * n + 3)
                    sp.sem_inc(sp_passed, 1)
                    for i, w in enumerate((w_gate, w_up, w_down)):
                        src = w.rearrange("a n -> (a n)").rearrange("(p n k) -> n p k", p=P, k=SCAN)
                        sp.dma_start(w_raw[:, i, :], src[n]).then_inc(scan_loaded, 16)

                def fill_stacks(v, par, r):
                    if not (isinstance(v, int) and v < 2):
                        sp.wait_ge(s_ready, EXPS * (2 * (v - 2) + r + 1))
                    for done, stack, parts in ((TG - 1, k_stack, (kT_hi, kT_hi, kT_lo)),
                                               (TG, q_stack, (qT_hi, qT_lo, qT_hi))):
                        sp.wait_ge(lo_ready, TG * v + done)
                        for j in (2 * r, 2 * r + 1):
                            for n, part in enumerate(parts):
                                sp.dma_start(stack[HD * n:HD * n + HD, 4 * par + j, :].bitcast(F32),
                                             part[HD * j:HD * j + HD, :].bitcast(F32)
                                             ).then_inc(stack_loaded[2 * par + r], 16)

                def free_kv(v):
                    sp.wait_ge(t_ready, TG * v + GROUPS)
                    sp.sem_inc(sp_passed, 1)
                    sp.wait_ge(v_ready, 2 * (v + 1))
                    sp.sem_inc(sp_passed, 1)

                load_kv(0, 0, 0)
                load_x(0)
                load_kv(0, 1, 1)
                fill_stacks(0, 0, 0)
                fill_stacks(0, 0, 1)
                for b in range(1, B):
                    load_x(b)
                free_kv(0)
                load_kv(0, 2, 0)
                fill_stacks(1, 1, 0)

                def period(it, c, more, left):
                    par, r = c // 2, c % 2
                    u = 2 * it + par
                    if r == 0 and (more or c == 0):
                        fill_stacks(u + 1, 1 - par, 1)
                    if c == 1:
                        scan_weights(it)
                    if r == 1 and more:
                        free_kv(u + 1)
                        if c == 1:
                            load_kv((it + 1) // 2, 2 * ((it + 1) % 2) + 1, 1)
                        else:
                            load_kv(((it + 2) // 2) % B, 2 * ((it + 2) % 2), 0)
                        fill_stacks(u + 2, par, 0)

                all_periods(sp, period)
                sp.wait_ge(scan_read, 24 + 3)
                for q in range(3):
                    load_piece(sp, q)
                sp.wait_ge(kv_loaded[0], 32 * (UNITS // 2 + 1))

            @block.gpsimd
            def _(pool):
                pool.memset(ident[:, :], 0.0)
                pool.memset(ident_b[:, :], 0.0)
                pool.memset(kT_hi[:, SK:SKP].bitcast(F32), 0.0)
                pool.memset(kT_lo[:, SK:SKP].bitcast(F32), 0.0)
                pool.memset(mask_k[:, :], 0.0)
                pool.memset(mask_q[:, :], 0.0).then_inc(consts_zero, 1)
                pool.wait_ge(consts_zero, 1)
                for m in (ident, ident_b):
                    pool.affine_select(out=m[:, :], in_=m[:, :], compare_op=ALU.not_equal, fill=1.0,
                                       base=0, pattern=[[-1, P]], channel_multiplier=1)
                pool.affine_select(out=mask_k[:, :], in_=mask_k[:, :], compare_op=ALU.is_gt, fill=MASKED,
                                   base=0, pattern=[[1, MASKW]], channel_multiplier=-1)
                pool.affine_select(out=mask_q[:, :], in_=mask_q[:, :], compare_op=ALU.is_gt, fill=MASKED,
                                   base=0, pattern=[[-1, P]], channel_multiplier=1).then_inc(consts_ready, 1)

                pool.memset(v_ones[:, :, :, :, :], 1.0)
                pool.memset(oT[:, :, :], 0.0).then_inc(consts_zero, 1)

                def copy_v(v, loads, par):
                    pool.wait_ge(kv_loaded[par], 32 * loads)
                    if not (isinstance(v, int) and v < 2):
                        pool.wait_ge(pv_done, 2 * EXPS * (v - 1) + P_RING)
                    pool.sem_inc(pool_passed, 1)
                    pool.tensor_copy(v_ones[:, par, 0:KT - 1, :, 0:HD],
                                     kv_sb[:, par, 0:KT - 1, :].rearrange("p t (h d) -> p t h d", h=HG)
                                     ).then_inc(v_ready, 1)
                    pool.tensor_copy(v_ones[0:KLAST, par, KT - 1, :, 0:HD],
                                     kv_sb[0:KLAST, par, KT - 1, :].rearrange("p (h d) -> p h d", h=HG)
                                     ).then_inc(v_ready, 1)

                pool.wait_ge(consts_zero, 2)
                pool.memset(k_stack[3 * HD:3 * HD + 1, :, :].bitcast(F32), 1.0).then_inc(ones_row, 1)
                pool.wait_ge(ones_row, 1)
                copy_v(0, 1, 0)

                def period(it, c, more, left):
                    par = c // 2
                    if c == 0 or (c == 2 and more):
                        copy_v(2 * it + par + 1, it + 1 + par, 1 - par)

                all_periods(pool, period)
                pool.wait_ge(amax_ready, 1)
                pool.partition_all_reduce(amax_all[:, :], amax[:, :], P, bass.bass_isa.ReduceOp.max
                                          ).then_inc(amax_shared, 1)

            @block.scalar
            def _(act):
                act.sem_inc(exp_done, S_BANKS)
                act.sem_inc(o_copied, 1)
                act.wait_ge(gates_loaded, 32)
                act.activation(tanhs[:, :], gates[:, :], ACT.Tanh).then_inc(tanh_ready, 1)

                def round_hi(v, i):
                    act.wait_ge(t_ready, TG * v + i + 1)
                    if i < GROUPS:
                        w = min(512, SK - 512 * i)
                        act.activation(kT_hi[:, 512 * i:512 * i + w], turn_bank(v, i)[:, 0:w], ACT.Copy).then_inc(hi_ready, 1)
                    else:
                        act.activation(qT_hi[:, :], turn_bank(v, i)[:, :], ACT.Copy).then_inc(hi_ready, 1)

                def copy_row(p, c, hh):
                    act.wait_ge(row_ready, 2 * p + hh + 1)
                    act.activation(q_stack[3 * HD:3 * HD + 1, 2 * c + hh, :], ps_m[3 * HD:3 * HD + 1, :],
                                   ACT.Copy).then_inc(row_copied, 1)

                def copy_o(p, c):
                    act.wait_ge(pv_done, EXPS * (p + 1) + P_RING)
                    act.wait_ge(ot_ready, p + 1)
                    act.activation(oT[:, c % 2, :], ps_o[0:64 + VW, :], ACT.Copy).then_inc(o_copied, 1)

                for i in range(TG):
                    round_hi(0, i)
                for i in (0, 1):
                    act.wait_ge(stack_loaded[i], 16 * STACK_DMAS)
                for i in range(TG):
                    round_hi(1, i)
                for hh in range(2):
                    copy_row(0, 0, hh)

                def period(it, c, more, left):
                    p = 4 * it + c
                    u = 2 * it + c // 2
                    for kt in range(KT):
                        K, w = key_rows(kt), SQ - q_start(kt)
                        for hh in range(2):
                            e = 2 * kt + hh
                            act.wait_ge(s_ready, EXPS * p + e + 1)
                            act.wait_ge(pv_done, EXPS * p + e + 1)
                            act.activation(probs[0:K, (EXPS * c + e) % P_RING, 0:w], score_bank(kt, hh, left)[0:K, 0:w],
                                           ACT.Exp, scale=SCALE).then_inc(exp_done, 1)
                        if kt == 0:
                            if not (isinstance(p, int) and p == 0):
                                copy_o(p - 1, (c + 3) % 4)
                        if more and kt in TURN_STEPS[c % 2]:
                            if TURN_STEPS[c % 2][kt] == 0:
                                for r in range(2):
                                    act.wait_ge(stack_loaded[2 * (1 - c // 2) + r],
                                                16 * STACK_DMAS * (it + 1 + c // 2))
                            round_hi(u + 2, TURN_STEPS[c % 2][kt])
                        if left and kt in row_steps(p):
                            copy_row(p + 1, (c + 1) % 4, row_steps(p).index(kt))

                all_periods(act, period)
                copy_o(4 * LOOPS + 3, 3)

            @block.vector
            def _(dve):
                dve.sem_inc(max_read, M_BANKS)
                dve.memset(ps_o[:, :], 0.0)
                dve.sem_inc(scan_read, 3)

                def unit_norms(turn, b):
                    dve.wait_ge(rstd_ready, turn + 1)
                    for dst, src in ((mean_u, mean), (rstd_u, rstd)):
                        dve.tensor_copy(
                            dst[:, :, :].rearrange("p (b g) t -> p b g t", b=B)[:, b],
                            src[:, b, :].unsqueeze(1).to_broadcast([P, G, QT])
                            ).then_inc(unit_stats, 1)

                def norm_q(v, par, tiles):
                    for t in tiles:
                        last = dve.tensor_scalar(xq[:, par, t, :], x_sb[:, v, t, :], mean_u[:, v, t:t + 1],
                                                 rstd_u[:, v, t:t + 1], ALU.subtract, ALU.mult)
                    if QT - 1 in tiles:
                        last.then_inc(xq_ready, 1)

                def rest_lo(v, i):
                    dve.wait_ge(hi_ready, TG * v + i + 1)
                    if i < GROUPS:
                        s = slice(512 * i, min(SK, 512 * i + 512))
                        dve.tensor_tensor(kT_lo[:, s], turn_bank(v, i)[:, 0:s.stop - s.start], kT_hi[:, s].bitcast(F32),
                                          ALU.subtract).then_inc(lo_ready, 1)
                    else:
                        dve.tensor_tensor(qT_lo[:, :], turn_bank(v, i)[:, :], qT_hi[:, :].bitcast(F32),
                                          ALU.subtract).then_inc(lo_ready, 1)

                def read_max(p, c, i):
                    hh, n = i // NCH, i % NCH
                    dve.wait_ge(max_scored, 2 * NCH * p + i + 1)
                    dve.tensor_reduce(max_part[:, c % 2, hh, n:n + 1], ps_max[i % M_BANKS][:, 0:CHUNKS[n][2]],
                                      AX.X, ALU.max).then_inc(max_read, 1)

                def join_max(p, c):
                    dve.wait_ge(max_read, 2 * NCH * (p + 1) + M_BANKS)
                    n, t = PER_T[0], PER_T.index(PER_T[-1])
                    dve.tensor_reduce(neg_max[:, c % 2, :, 0:t],
                                      max_part[:, c % 2, :, 0:n * t].rearrange("p h (t n) -> p h t n", n=n),
                                      AX.X, ALU.max, negate=True).then_inc(neg_ready, 1)
                    dve.tensor_reduce(neg_max[:, c % 2, :, t:QT],
                                      max_part[:, c % 2, :, n * t:NCH].rearrange("p h (t n) -> p h t n", t=QT - t),
                                      AX.X, ALU.max, negate=True).then_inc(neg_ready, 1)

                def add_attention(p, c, u):
                    o = ps_m[:, :].rearrange("p (t w) -> p t w", t=QT)
                    dve.wait_ge(ot_ready, p + 3)
                    dve.reciprocal(den_inv[:, :, :], o[:, :, HD:HD + 65:64]).then_inc(tail_chain, 1)
                    dve.wait_ge(tail_chain, 2 * p + 1)
                    for hh in range(2):
                        last = dve.scalar_tensor_tensor(
                            att[:, :, hh, :], o[:, :, 64 * hh:64 * hh + HD], tanhs[:, 0:1],
                            den_inv[:, :, hh:hh + 1].to_broadcast([P, QT, HD]), ALU.mult, ALU.mult)
                    last.then_inc(tail_chain, 1)
                    dve.wait_ge(tail_chain, 2 * p + 2)
                    xs = x_sb[:, u, :, 64 * (c % 2):64 * (c % 2) + 64]
                    dve.tensor_tensor(xs, xs, att[:, :, :, :].rearrange("p t h d -> p t (h d)"),
                                      ALU.add).then_inc(x_added, 1)

                for i in range(GROUPS):
                    rest_lo(0, i)
                dve.wait_ge(x_loaded[0], 16 * G)
                for i in range(NORM_PARTS):
                    norm_part(dve, 0, 0, i)
                unit_norms(0, 0)
                dve.wait_ge(unit_stats, 2)
                norm_q(0, 0, range(QT))
                rest_lo(0, GROUPS)
                for i in range(2 * NCH):
                    read_max(0, 0, i)
                    if i < QT:
                        norm_q(1, 1, (i,))
                    if i in START_CHUNKS:
                        rest_lo(1, START_CHUNKS[i])
                join_max(0, 0)
                dve.wait_ge(tanh_ready, 1)

                NORM_STEPS = [4, 6, 7, 9]

                def read_scan(n, i):
                    dve.wait_ge(scan_loaded, 48 * (n + 1))
                    dve.tensor_reduce(amax_part[:, i, n, :], w_raw[:, i, :], AX.X, ALU.max,
                                      apply_absolute_value=True).then_inc(scan_read, 1)

                def join_scans():
                    dve.wait_ge(scan_read, 24 + 3)
                    dve.tensor_reduce(amax[:, :], amax_part[:, :, :, 0], AX.X, ALU.max).then_inc(amax_ready, 1)

                def weight_scales():
                    dve.wait_ge(amax_shared, 1)
                    dve.tensor_scalar(amax[:, :], amax_all[:, :], 1e-30, None, ALU.max).then_inc(scale_chain, 1)
                    dve.wait_ge(scale_chain, 1)
                    dve.tensor_scalar(pow2[:, :].bitcast(U32), amax[:, :].bitcast(U32), 0x7F800000, None,
                                      ALU.bitwise_and).then_inc(scale_chain, 1)
                    dve.wait_ge(scale_chain, 2)
                    dve.tensor_scalar(inv_scale[:, :], pow2[:, :], 2.0 ** -14, None, ALU.mult
                                      ).then_inc(scale_chain, 1)
                    dve.wait_ge(scale_chain, 3)
                    dve.reciprocal(w_scale[:, :], inv_scale[:, :]).then_inc(scale_chain, 1)

                def period(it, c, more, left):
                    p = 4 * it + c
                    u = 2 * it + c // 2
                    if c == 2 and not more:
                        join_scans()
                    if c == 3 and not more:
                        weight_scales()
                        for i in range(NORM_PARTS):
                            norm_part(dve, LOOPS + 1, B - 2, i)
                    for kt in range(KT):
                        if left and kt == join_step(p):
                            join_max(p + 1, (c + 1) % 4)
                        for chunk in chunks_at(p, c, kt, left):
                            read_max(*chunk)
                        if kt == 2:
                            prev = 2 * it - 1 if c == 0 else 2 * it + (c - 1) // 2
                            if not (isinstance(p, int) and p == 0):
                                add_attention(p - 1, (c + 3) % 4, prev)
                        if more and kt in TURN_STEPS[c % 2]:
                            rest_lo(u + 2, TURN_STEPS[c % 2][kt])
                        if c % 2 == 0 and more and kt in NORM_STEPS:
                            if kt == NORM_STEPS[0]:
                                dve.wait_ge(unit_stats, 2 * ((it + 1) // 2 + 1) if not isinstance(it, int) else 2)
                            norm_q((u + 2) % UNITS, c // 2, (NORM_STEPS.index(kt),))
                        if c == 1 and kt in (6, 8, 10):
                            read_scan(it, (6, 8, 10).index(kt))
                        if c == 3 and more and 0 <= kt - 3 < NORM_PARTS:
                            if kt == 3:
                                dve.wait_ge(x_loaded[1], 16 * G * (B - 1))
                                dve.wait_ge(x_added, p)
                                dve.sem_inc(dve_passed, 1)
                            norm_part(dve, it + 1, (it + 1) % B, kt - 3)
                        if c == 3 and more and kt == 3 + NORM_PARTS:
                            unit_norms(it + 1, (it + 1) % B)

                all_periods(dve, period)
                add_attention(4 * LOOPS + 3, 3, 2 * LOOPS + 1)

            @block.tensor
            def _(pe):
                pe.sem_inc(pv_done, P_RING)
                pe.sem_inc(ot_ready, 2)
                pe.wait_ge(consts_ready, 1)

                def turn(v, loads, par, i):
                    bank = turn_bank(v, i)
                    if not (isinstance(v, int) and v < 2):
                        pe.wait_ge(lo_ready, TG * v + i)
                    elif i == TG - 1 or v == 1:
                        pe.wait_ge(lo_ready, TG * v + 1 if i == TG - 1 else TG)
                    if i < GROUPS:
                        pe.wait_ge(kv_loaded[par], 32 * loads)
                        for t in range(4 * i, min(KT, 4 * i + 4)):
                            K = key_rows(t)
                            last = pe.transpose(bank[:, P * (t % 4):P * (t % 4) + K], kv_sb[0:K, par, t, :],
                                                ident[0:K, 0:K])
                    else:
                        pe.wait_ge(xq_ready, v + 1)
                        for t in range(QT):
                            last = pe.transpose(bank[:, P * t:P * t + P], xq[:, par, t, :], ident[:, :])
                    last.then_inc(t_ready, 1)

                def score_max(p, c, i):
                    hh, n = i // NCH, i % NCH
                    t, a, w = CHUNKS[n]
                    bank = ps_max[i % M_BANKS]
                    pe.wait_ge(max_read, max_reads_before(p, i))
                    masked = n + 1 == NCH or CHUNKS[n + 1][0] != t
                    last = pe.matmul(bank[:, 0:w], q_stack[0:3 * HD, 2 * c + hh, P * t:P * t + P],
                                     k_stack[0:3 * HD, 2 * c + hh, a:a + w], start=True, stop=True)
                    if masked:
                        last = pe.matmul(bank[:, w - P:w], ident_b[:, :], mask_q[:, :], start=False, stop=True,
                                         skip_group_check=True)
                    last.then_inc(max_scored, 1)

                def max_row(p, c, hh):
                    pe.wait_ge(neg_ready, 2 * (p + 1))
                    for t in range(QT):
                        last = pe.matmul(ps_m[3 * HD:3 * HD + 1, P * t:P * t + P], neg_max[:, c % 2, hh, t:t + 1],
                                         ident_b[:, :], start=True, stop=True)
                    last.then_inc(row_ready, 1)

                def score(p, c, kt, hh, left):
                    K, q0, slot = key_rows(kt), q_start(kt), 2 * c + hh
                    bank = score_bank(kt, hh, left)
                    e = 2 * kt + hh
                    if left == 2 or (left == 1 and e < 4):
                        pe.wait_ge(exp_done, EXPS * p + e + 1)
                        if left == 1 and e == 2:
                            pe.wait_ge(max_read, 8 * NCH * (LOOPS + 1) + M_BANKS)
                    else:
                        pe.wait_ge(exp_done, EXPS * p + e - 1)
                    d = diagonal(kt)
                    last = pe.matmul(bank[0:K, 0:SQ - q0], k_stack[:, slot, P * kt:P * kt + K],
                                     q_stack[:, slot, q0:SQ], start=True, stop=True)
                    if d:
                        m0, w = d
                        last = pe.matmul(bank[0:K, 0:w], ident_b[0:K, 0:K], mask_k[0:K, m0:m0 + w],
                                         start=False, stop=True, skip_group_check=True)
                    last.then_inc(s_ready, 1)

                def values(p, c, kt, hh, unit=None):
                    K, q0, e = key_rows(kt), q_start(kt), 2 * kt + hh
                    pe.wait_ge(exp_done, EXPS * p + e + 1 + S_BANKS)
                    if kt == 0 and hh == 0:
                        pe.wait_ge(o_copied, p + 1)
                        pe.wait_ge(v_ready, 2 * unit + 2)
                    pe.matmul(ps_o[64 * hh:64 * hh + VW, q0:SQ],
                              v_ones[0:K, c // 2, kt, 2 * (c % 2) + hh, 0:VW],
                              probs[0:K, (EXPS * c + e) % P_RING, 0:SQ - q0],
                              start=kt == 0, stop=kt == KT - 1, skip_group_check=True).then_inc(pv_done, 1)

                def turn_o(p, c):
                    pe.wait_ge(o_copied, p + 2)
                    for t in range(QT):
                        last = pe.transpose(ps_m[:, P * t:P * t + 64 + VW], oT[:, c % 2, P * t:P * t + P],
                                            ident[0:64 + VW, 0:64 + VW])
                    last.then_inc(ot_ready, 1)

                for i in range(TG):
                    turn(0, 1, 0, i)
                pe.wait_ge(stack_loaded[0], 16 * STACK_DMAS)
                for i in range(2 * NCH):
                    score_max(0, 0, i)
                    if i in START_CHUNKS:
                        turn(1, 1, 1, START_CHUNKS[i])
                pe.wait_ge(ones_row, 1)
                pe.wait_ge(lo_ready, 2 * TG)
                max_row(0, 0, 0)
                pe.wait_ge(row_copied, 1)
                max_row(0, 0, 1)

                def period(it, c, more, left):
                    p = 4 * it + c
                    u = 2 * it + c // 2
                    first = isinstance(p, int) and p == 0
                    if left == 2:
                        if first:
                            pe.wait_ge(stack_loaded[1], 16 * STACK_DMAS)
                        else:
                            pe.wait_ge(stack_loaded[(c + 2) % 4], 16 * STACK_DMAS * (it + 1 + c // 2))
                    for kt in range(KT):
                        chunks = chunks_at(p, c, kt, left)
                        half = len(chunks) // 2
                        if kt == 0:
                            pe.wait_ge(row_copied, 2 * (p + 1))
                        score(p, c, kt, 0, left)
                        for chunk in chunks[:half]:
                            if first and chunk[0] == 2 and chunk[2] == 0:
                                pe.wait_ge(stack_loaded[2], 16 * STACK_DMAS)
                            score_max(*chunk)
                        score(p, c, kt, 1, left)
                        if more and kt in TURN_STEPS[c % 2]:
                            turn(u + 2, it + 2, c // 2, TURN_STEPS[c % 2][kt])
                        if kt == 2 and not first:
                            turn_o(p - 1, (c + 3) % 4)
                        if left and kt == row_steps(p)[0]:
                            if not first:
                                pe.wait_ge(x_added, p)
                            max_row(p + 1, (c + 1) % 4, 0)
                        if left and kt == row_steps(p)[1]:
                            pe.wait_ge(row_copied, 2 * (p + 1) + 1)
                            max_row(p + 1, (c + 1) % 4, 1)
                        for hh in range(2):
                            if kt > 0:
                                values(p, c, kt - 1, hh, u)
                            elif not first:
                                values(p - 1, (c + 3) % 4, KT - 1, hh)
                        for chunk in chunks[half:]:
                            if first and chunk[0] == 2 and chunk[2] == 0:
                                pe.wait_ge(stack_loaded[2], 16 * STACK_DMAS)
                            score_max(*chunk)

                all_periods(pe, period)
                p = 4 * LOOPS + 3
                for hh in range(2):
                    values(p, 3, KT - 1, hh)
                pe.wait_ge(x_added, p)
                turn_o(p, 3)

        with ExitStack() as ctx:
            def sb(name, shape, dt=F32):
                return ctx.enter_context(nc.sbuf_tensor(name, shape, dt))

            def pb(name, shape, dt=F32):
                return ctx.enter_context(nc.psum_tensor(name, shape, dt))

            IT = JB * M
            X_SCALE = 256.0
            HID_SCALE = 2.0 ** -50

            wg_hi, wg_lo, wu_hi, wu_lo = (sb(n, [P, G, INNER], F16) for n in ("wg_hi", "wg_lo", "wu_hi", "wu_lo"))
            wd_hi, wd_lo = (sb(n, [P, JB, M, D], F16) for n in ("wd_hi", "wd_lo"))
            xn = sb("xn", [P, QT, G, P])
            xT_hi = sb("xT_hi", [P, G, SQ], F16)
            xT_lo = sb("xT_lo", [P, G, SQ], F16)
            silu = sb("silu", [P, 2, SQ])
            hid = sb("hid", [P, 2, SQ])
            mag = sb("mag", [P, M, SQ])
            hid_hi = sb("hid_hi", [P, M, SQ], F16)
            hid_lo = sb("hid_lo", [P, M, SQ], F16)
            beats = sb("beats", [P, 6, SQ], F16)
            wins = sb("wins", [P, M, SQ], F16)
            kept_hi = sb("kept_hi", [P, M, SQ], F16)
            kept_lo = sb("kept_lo", [P, M, SQ], F16)
            tanh_scale = sb("tanh_scale", [P, 1])
            out_scale = sb("out_scale", [P, 1])

            ps_g = [pb(f"ps_g{i}", [P, 512]) for i in range(2)]
            ps_u = [pb(f"ps_u{i}", [P, 512]) for i in range(2)]
            ps_d = [pb(f"ps_d{i}", [P, 512]) for i in range(QT)]

            w_round = sem("w_round")
            factors = sem("factors")
            xn_ready = sem("xn_ready")
            xt_turned = sem("xt_turned")
            xt_hi_ready = sem("xt_hi_ready")
            xt_lo_ready = sem("xt_lo_ready")
            gate_ready = sem("gate_ready")
            up_ready = sem("up_ready")
            tanh_done = sem("tanh_done")
            silu_ready = sem("silu_ready")
            hid_ready = sem("hid_ready")
            mag_ready = sem("mag_ready")
            hid_hi_ready = sem("hid_hi_ready")
            hid_lo_ready = sem("hid_lo_ready")
            beats_ready = sem("beats_ready")
            wins_ready = sem("wins_ready")
            kept_ready = sem("kept_ready")
            down_ready = sem("down_ready")
            kept_used = sem("kept_used")
            y_ready = sem("y_ready")
            y_stored = sem("y_stored")

            block = ctx.enter_context(nc.Block())

            def weights_of(q):
                j, kind, half = *ORDER[q // 2], q % 2
                if kind < 2:
                    hi, lo = ((wg_hi, wg_lo), (wu_hi, wu_lo))[kind]
                    return kind, *(w[:, 2 * half:2 * half + 2, SQ * j:SQ * j + SQ] for w in (hi, lo))
                return kind, *(w[:, j, 2 * half:2 * half + 2, :] for w in (wd_hi, wd_lo))

            def raw(q):
                return w_raw[:, q % 3, :].rearrange("p (a n) -> p a n", a=2)

            def pieces_after(i):
                j, m = i // M, i % M
                q = 4 + 6 * j + 2 * (m - 1)
                return range(q, q + 2) if m < 3 and 4 <= q < PIECES else ()

            def all_batches(eng, batch):
                batch(0)
                with eng.Fori(1, B - 1) as b:
                    batch(b)
                batch(B - 1)

            def is_batch(b, n):
                return isinstance(b, int) and b == n

            XT_BANKS = [ps_g[0], ps_u[0], ps_g[1], ps_u[1]]

            @block.sync
            def _(sp):
                for q in range(3, PIECES):
                    load_piece(sp, q)

                def store(b):
                    for t in range(QT):
                        sp.wait_ge(y_ready, QT * b + t + 1)
                        sp.sem_inc(sp_passed, 1)
                        xv = x_sb[:, :, t, :].rearrange("p (b g) d -> p b g d", b=B)
                        sp.dma_start(out_v[b, t].rearrange("p (g d) -> p g d", g=G), xv[:, b]).then_inc(y_stored, 16)

                with sp.Fori(0, B) as b:
                    store(b)
                sp.wait_ge(y_stored, 16 * B * QT)

            @block.scalar
            def _(act):
                def split(q):
                    kind, hi, _lo = weights_of(q)
                    act.wait_ge(w_loaded[q % 3], 16 * (q // 3 + 1))
                    act.activation(hi, raw(q), ACT.Copy, scale=w_scale[:, kind:kind + 1]).then_inc(w_round, 1)

                def turned_hi(b):
                    for c in range(G):
                        act.wait_ge(xt_turned, G * b + c + 1)
                        if c == 0 and not is_batch(b, 0):
                            act.wait_ge(up_ready, IT * b)
                        act.activation(xT_hi[:, c, :], XT_BANKS[c][:, :], ACT.Copy, scale=X_SCALE
                                       ).then_inc(xt_hi_ready, 1)

                def batch(b):
                    first = is_batch(b, 0)
                    if first:
                        for q in (0, 1):
                            split(q)
                        turned_hi(0)
                        for q in (2, 3):
                            split(q)
                        act.wait_ge(factors, 2)
                    for i in range(IT):
                        n = IT * b + i
                        s = i % 2
                        act.wait_ge(gate_ready, n + 1)
                        if not (first and i < 2):
                            act.wait_ge(hid_ready, n - 1)
                        act.activation(silu[:, s, :], ps_g[s][:, :], ACT.Tanh, scale=tanh_scale[:, 0:1]
                                       ).then_inc(tanh_done, 1)
                        act.wait_ge(hid_ready, n + 1)
                        if i % M == 0 and not (first and i == 0):
                            act.wait_ge(kept_ready, JB * b + i // M)
                        act.activation(mag[:, i % M, :], hid[:, s, :], ACT.Abs).then_inc(mag_ready, 1)
                        act.activation(hid_hi[:, i % M, :], hid[:, s, :], ACT.Copy).then_inc(hid_hi_ready, 1)
                        if first:
                            for q in pieces_after(i):
                                split(q)

                    if not is_batch(b, B - 1):
                        turned_hi(b + 1)

                all_batches(act, batch)

            @block.vector
            def _(dve):
                def norm_tokens(b, tiles):
                    if 0 in tiles and not is_batch(b, 0):
                        dve.wait_ge(xt_turned, G * b)
                    for t in tiles:
                        dve.tensor_scalar(xn[:, t, :, :],
                                          x_sb[:, :, t, :].rearrange("p (b g) d -> p b g d", b=B)[:, b],
                                          mean[:, b, t:t + 1], rstd[:, b, t:t + 1], ALU.subtract, ALU.mult).then_inc(xn_ready, 1)

                def turned_lo(b):
                    for c in range(G):
                        dve.wait_ge(xt_hi_ready, G * b + c + 1)
                        dve.scalar_tensor_tensor(xT_lo[:, c, :], XT_BANKS[c][:, :], X_SCALE, xT_hi[:, c, :],
                                                 ALU.mult, ALU.subtract).then_inc(xt_lo_ready, 1)

                def split(q):
                    kind, hi, lo = weights_of(q)
                    dve.wait_ge(w_round, q + 1)
                    dve.scalar_tensor_tensor(lo, raw(q), w_scale[:, kind:kind + 1], hi, ALU.mult, ALU.subtract
                                             ).then_inc(w_rest, 1)

                def select(k):
                    dve.wait_ge(mag_ready, M * (k + 1))
                    dve.tensor_tensor(beats[:, 0:3, :], mag[:, 0:3, :], mag[:, 1:4, :], ALU.is_ge)
                    dve.tensor_tensor(beats[:, 3:5, :], mag[:, 0:2, :], mag[:, 2:4, :], ALU.is_ge)
                    dve.tensor_tensor(beats[:, 5, :], mag[:, 0, :], mag[:, 3, :], ALU.is_ge
                                      ).then_inc(beats_ready, 1)
                    dve.wait_ge(beats_ready, k + 1)
                    dve.tensor_tensor(wins[:, 0:2, :], beats[:, 0:2, :], beats[:, 3:5, :], ALU.add)
                    dve.tensor_tensor(wins[:, 2, :], beats[:, 2, :], beats[:, 3, :], ALU.subtract)
                    dve.tensor_tensor(wins[:, 3, :], beats[:, 2, :], beats[:, 4, :], ALU.add
                                      ).then_inc(wins_ready, 1)
                    dve.wait_ge(wins_ready, 3 * k + 1)
                    dve.tensor_tensor(wins[:, 1:3, :], wins[:, 1:3, :], beats[:, 0:2, :], ALU.subtract)
                    dve.tensor_tensor(wins[:, 0, :], wins[:, 0, :], beats[:, 5, :], ALU.add)
                    dve.tensor_tensor(wins[:, 3, :], wins[:, 3, :], beats[:, 5, :], ALU.add
                                      ).then_inc(wins_ready, 1)
                    dve.wait_ge(wins_ready, 3 * k + 2)
                    for m, (least, op) in enumerate(((1.5, ALU.is_gt), (0.5, ALU.is_gt), (-0.5, ALU.is_gt),
                                                     (1.5, ALU.is_lt))):
                        last = dve.tensor_scalar(wins[:, m, :], wins[:, m, :], least, None, op)
                    last.then_inc(wins_ready, 1)
                    dve.wait_ge(wins_ready, 3 * k + 3)
                    dve.wait_ge(hid_lo_ready, M * (k + 1))
                    if not (isinstance(k, int) and k == 0):
                        dve.wait_ge(kept_used, k)
                    dve.tensor_tensor(kept_hi[:, :, :], hid_hi[:, :, :], wins[:, :, :], ALU.mult)
                    dve.tensor_tensor(kept_lo[:, :, :], hid_lo[:, :, :], wins[:, :, :], ALU.mult
                                      ).then_inc(kept_ready, 1)

                def add_down(b, tiles):
                    for t in tiles:
                        dve.wait_ge(down_ready, QT * b + t + 1)
                        xv = x_sb[:, :, t, :].rearrange("p (b g) d -> p b g d", b=B)[:, b]
                        dve.scalar_tensor_tensor(xv, ps_d[t][:, :].rearrange("p (g d) -> p g d", g=G),
                                                 out_scale[:, 0:1], xv, ALU.mult, ALU.add).then_inc(y_ready, 1)

                def batch(b):
                    first = is_batch(b, 0)
                    if first:
                        norm_tokens(0, range(QT))
                        for q in (0, 1):
                            split(q)
                        turned_lo(0)
                        for q in (2, 3):
                            split(q)
                    for i in range(IT):
                        n = IT * b + i
                        s = i % 2
                        dve.wait_ge(tanh_done, n + 1)
                        dve.scalar_tensor_tensor(silu[:, s, :], silu[:, s, :], 1.0, ps_g[s][:, :],
                                                 ALU.add, ALU.mult).then_inc(silu_ready, 1)
                        dve.wait_ge(silu_ready, n + 1)
                        dve.wait_ge(up_ready, n + 1)
                        if not (first and i < 2):
                            dve.wait_ge(hid_lo_ready, n - 1)
                        dve.scalar_tensor_tensor(hid[:, s, :], silu[:, s, :], HID_SCALE, ps_u[s][:, :],
                                                 ALU.mult, ALU.mult).then_inc(hid_ready, 1)
                        dve.wait_ge(hid_hi_ready, n + 1)
                        dve.tensor_tensor(hid_lo[:, i % M, :], hid[:, s, :], hid_hi[:, i % M, :],
                                          ALU.subtract).then_inc(hid_lo_ready, 1)
                        if first:
                            for q in pieces_after(i):
                                split(q)
                        if first and i == STATS_TILE:
                            for part in range(NORM_PARTS):
                                norm_part(dve, LOOPS + 2, B - 1, part)
                        if not first and i in ADD_TILES:
                            add_down(b - 1, ADD_TILES[i])
                        if not is_batch(b, B - 1) and i in NORM_TILES:
                            norm_tokens(b + 1, NORM_TILES[i])
                        if i == IT - 1 and not is_batch(b, B - 1):
                            turned_lo(b + 1)
                        if i % M == M - 1:
                            select(JB * b + i // M)

                STATS_TILE = 10
                ADD_TILES = {2: (0, 1), 4: (2,), 5: (3,)}
                NORM_TILES = {12: (0, 1), 13: (2, 3)}
                dve.tensor_scalar(tanh_scale[:, :], inv_scale[:, 0:1], 0.5 / X_SCALE, None, ALU.mult
                                  ).then_inc(factors, 1)
                dve.tensor_scalar(out_scale[:, :], inv_scale[:, 0:1], inv_scale[:, 1:2],
                                  0.5 / (X_SCALE * X_SCALE * HID_SCALE), ALU.mult, ALU.mult).then_inc(factors, 1)
                dve.wait_ge(factors, 2)
                dve.tensor_scalar(out_scale[:, :], out_scale[:, :], inv_scale[:, 2:3], tanhs[:, 1:2],
                                  ALU.mult, ALU.mult).then_inc(factors, 1)
                dve.wait_ge(factors, 3)
                all_batches(dve, batch)
                add_down(B - 1, range(QT))

            @block.tensor
            def _(pe):
                def down(b, j, behind=None):
                    k = JB * b + j
                    pe.wait_ge(kept_ready, k + 1)
                    if j == 0 and not is_batch(b, 0):
                        pe.wait_ge(y_ready, QT * b)
                    for t in range(QT):
                        if t == 2 and behind:
                            behind()
                        rows = slice(P * t, P * t + P)
                        for m in range(M):
                            for n, (a, w) in enumerate(((kept_hi, wd_hi), (kept_hi, wd_lo), (kept_lo, wd_hi))):
                                last = pe.matmul(ps_d[t][:, :], a[:, m, rows], w[:, j, m, :],
                                                 start=(j == 0 and m == 0 and n == 0),
                                                 stop=(j == JB - 1 and m == M - 1 and n == 2))
                        if j == JB - 1:
                            last.then_inc(down_ready, 1)
                        elif t == QT - 1:
                            last.then_inc(kept_used, 1)
                    if j == JB - 1:
                        pe.sem_inc(kept_used, 1)

                def turn_x(b):
                    pe.wait_ge(xn_ready, QT * (b + 1))
                    for c in range(G):
                        if not is_batch(b, 0):
                            pe.wait_ge(hid_ready if c % 2 else silu_ready, IT * b - 1 + c // 2)
                        for t in range(QT):
                            last = pe.transpose(XT_BANKS[c][:, P * t:P * t + P], xn[:, t, c, :], ident[:, :])
                        last.then_inc(xt_turned, 1)

                def batch(b):
                    first = is_batch(b, 0)
                    if first:
                        turn_x(0)
                    pe.wait_ge(xt_lo_ready, G * (b + 1))
                    for i in range(IT):
                        j, m = i // M, i % M
                        n = IT * b + i
                        s = i % 2
                        if first and m == 0:
                            pe.wait_ge(w_rest, 6 * j + 2 - (2 if j else 0))
                        for w_hi, w_lo, bank, read, ready in ((wg_hi, wg_lo, ps_g[s], silu_ready, gate_ready),
                                                              (wu_hi, wu_lo, ps_u[s], hid_ready, up_ready)):
                            if not (first and i < 2):
                                pe.wait_ge(read, n - 1)
                            if first and m == 0 and bank is ps_u[0]:
                                pe.wait_ge(w_rest, 6 * j + 4 - (2 if j else 0))
                            cols = slice(SQ * j + m, SQ * j + SQ, M)
                            for c in range(G):
                                for k, (w, xx) in enumerate(((w_hi, xT_hi), (w_hi, xT_lo), (w_lo, xT_hi))):
                                    last = pe.matmul(bank[:, :], w[:, c, cols], xx[:, c, :],
                                                     start=c == 0 and k == 0, stop=c == G - 1 and k == 2)
                            last.then_inc(ready, 1)
                        if i == 1 and not first:
                            pe.wait_ge(w_rest, PIECES)
                            down(b - 1, JB - 1)
                        if m == M - 1 and j > 0:
                            if first:
                                pe.wait_ge(w_rest, 6 * j + 4)
                            last_block = j == JB - 1 and not is_batch(b, B - 1)
                            down(b, j - 1, (lambda: turn_x(b + 1)) if last_block else None)

                all_batches(pe, batch)
                down(B - 1, JB - 1)


_INS = ["x", "ctx_2048", "g_xattn", "g_ffn", "L0_ffn_w_gate", "L0_ffn_w_up", "L0_ffn_w_down"]


def kernel(**inputs):
    import numpy as _np
    import concourse.bacc as _bacc
    from concourse import mybir as _mybir
    from concourse.bass_utils import run_bass_kernel_spmd as _run

    nc = _bacc.Bacc("TRN2", target_bir_lowering=False, num_devices=1)
    arrays, args = {}, []
    for name in _INS:
        a = _np.ascontiguousarray(inputs[name])
        arrays[f"in_{name}_dram"] = a
        args.append(nc.dram_tensor(f"in_{name}_dram", a.shape, _mybir.dt.from_np(a.dtype), kind="ExternalInput").ap())
    shape = _np.asarray(inputs["x"]).shape
    y = nc.dram_tensor("out_0_dram", shape, _mybir.dt.float32, kind="ExternalOutput").ap()
    gated_cross_attention_ffn(nc, *args, y)
    r = _run(nc, [arrays], core_ids=[0])
    return r.results[0]["out_0_dram"]
```

```python
from contextlib import ExitStack

import concourse.bass as bass
from concourse import mybir

F32 = mybir.dt.float32
F32R = mybir.dt.float32r
BF16 = mybir.dt.bfloat16
F16 = mybir.dt.float16
U32 = mybir.dt.uint32
ALU = mybir.AluOpType
ACT = mybir.ActivationFunctionType
AX = mybir.AxisListType

P = 128
HEADS = 16
HD = 32
EPS = 1e-5
MASKED = -1e30
S_BANKS = 2
M_BANKS = 3
P_RING = 8


def gated_cross_attention_ffn(nc, x, ctx_kv, g_xattn, g_ffn, w_gate, w_up, w_down, out):
    B, SQ, D = x.shape
    SK = ctx_kv.shape[1]
    INNER = w_gate.shape[1]
    QT = SQ // P
    HG = P // HD
    G = D // P
    UNITS = B * G
    KT = -(-SK // P)
    KLAST = SK - (KT - 1) * P
    SHIFT = SK - SQ
    SKP = SK + SK % 2
    SCALE = float(HD) ** -0.5
    VW = HD + 1

    def q_start(kt):
        return max(0, (P * kt - SHIFT) // 2 * 2)

    def key_rows(kt):
        return KLAST if kt == KT - 1 else P

    def diagonal(kt):
        c0 = q_start(kt) - (P * kt - SHIFT) + 1
        w = min(P - c0, SQ - q_start(kt))
        return (c0, w + w % 2) if w > 0 else None

    def max_chunks(t):
        end = SHIFT + P * t + P + 1
        end += end % 2
        cuts = list(range(0, end, 512)) + [end]
        if cuts[-2] > end - P:
            cuts[-2] = end - P
        return [(a, b - a) for a, b in zip(cuts, cuts[1:])]

    CHUNKS = [(t, a, w) for t in range(QT) for a, w in max_chunks(t)]
    NCH = len(CHUNKS)
    PER_T = [len(max_chunks(t)) for t in range(QT)]
    MASKED_TILES = 2 * sum(diagonal(kt) is not None for kt in range(KT))
    EXPS = 2 * KT
    GROUPS = -(-KT // 4)
    TG = GROUPS + 1
    STACK_DMAS = 2 * 3 * 2
    SCAN = G * INNER // 8

    x_v = x.rearrange("b (t p) (g d) -> p b g t d", p=P, g=G)
    ctx_v = ctx_kv.rearrange("b s (g d) -> b g s d", g=G)
    out_v = out.rearrange("b (t p) d -> b t p d", p=P)

    with ExitStack() as outer:
        def sem(name):
            return outer.enter_context(nc.semaphore(name))

        def keep(name, shape, dt=F32):
            return outer.enter_context(nc.sbuf_tensor(name, shape, dt))

        x_sb = keep("x_sb", [P, UNITS, QT, P])
        ident = keep("ident", [P, P])
        gates = keep("gates", [P, 2])
        tanhs = keep("tanhs", [P, 2])
        stats = keep("stats", [P, QT, 6])
        mv = keep("mv", [P, QT, 2])
        var = keep("var", [P, QT])
        root = keep("root", [P, QT])
        tmp_s = keep("tmp_s", [P, QT])
        mean = keep("mean", [P, B, QT])
        rstd = keep("rstd", [P, B, QT])
        xn = keep("xn", [P, QT, G, P])
        w_raw = keep("w_raw", [P, 3, SCAN])
        inv_scale = keep("inv_scale", [P, 3])
        w_scale = keep("w_scale", [P, 3])
        w_loaded = [sem(f"w_loaded{i}") for i in range(3)]
        xn_ready = sem("xn_ready")
        ln_chain = sem("ln_chain")
        rstd_ready = sem("rstd_ready")
        gates_loaded = sem("gates_loaded")
        tanh_ready = sem("tanh_ready")
        x_loaded = [sem("x_loaded_first"), sem("x_loaded_rest")]
        sp_passed = sem("sp_passed")
        pool_passed = sem("pool_passed")
        dve_passed = sem("dve_passed")
        act_passed = sem("act_passed")

        NORM_PARTS = QT + 4
        NORM_LINKS = [0] * QT + [1, 6, 9, 12, 14]

        def norm_part(dve, turn, b, i):
            done = [NORM_LINKS[-1] * turn + NORM_LINKS[i]]
            v, y, t = (w[:, :] for w in (var, root, tmp_s))

            def link(ins):
                ins.then_inc(ln_chain, 1)
                done[0] += 1
                dve.wait_ge(ln_chain, done[0])

            if i < QT:
                xs = x_sb[:, :, i, :].rearrange("p (b g) d -> p b g d", b=B)[:, b]
                last = dve.bn_stats(stats[:, i, :], xs)
                if i == QT - 1:
                    link(last)
                    dve.sem_inc(dve_passed, 1)
            elif i == QT:
                for n in range(QT):
                    last = dve.bn_aggr(mv[:, n, :], stats[:, n, :])
                link(last)
                dve.tensor_copy(mean[:, b, :], mv[:, :, 0])
                link(dve.tensor_scalar(v, mv[:, :, 1], EPS, None, ALU.add))
                link(dve.reciprocal(t, v))
                link(dve.tensor_scalar(t.bitcast(U32), t.bitcast(U32), 1, None, ALU.logical_shift_right))
                link(dve.tensor_scalar(y, t, 0.97 * 2.0 ** 63.5, None, ALU.mult))
            else:
                link(dve.tensor_tensor(t, y, y, ALU.mult))
                link(dve.scalar_tensor_tensor(t, t, -0.5, v, ALU.mult, ALU.mult))
                if i < NORM_PARTS - 1:
                    link(dve.scalar_tensor_tensor(y, t, 1.5, y, ALU.add, ALU.mult))
                else:
                    dve.scalar_tensor_tensor(rstd[:, b, :], t, 1.5, y, ALU.add, ALU.mult).then_inc(rstd_ready, 1)

        def norm_tokens(dve, b, tiles):
            for t in tiles:
                dve.tensor_scalar(xn[:, t, :, :], x_sb[:, :, t, :].rearrange("p (b g) d -> p b g d", b=B)[:, b],
                                  mean[:, b, t:t + 1], rstd[:, b, t:t + 1], ALU.subtract, ALU.mult
                                  ).then_inc(xn_ready, 1)

        JB = INNER // SQ
        M = 4
        PIECES = 6 * JB

        ORDER = [(0, 0), (0, 1), *((j - k // 2, k) for j in range(1, JB) for k in range(3)), (JB - 1, 2)]
        w_rest = sem("w_rest")
        wd_rest = sem("wd_rest")

        def wait_split(eng, q):
            down = ORDER[q // 2][1] == 2
            count = sum((ORDER[n // 2][1] == 2) == down for n in range(q + 1))
            eng.wait_ge(wd_rest if down else w_rest, count)

        def load_piece(sp, q):
            j, kind, half = *ORDER[q // 2], q % 2
            if q >= 3:
                wait_split(sp, q - 3)
            dst = w_raw[:, q % 3, :].rearrange("p (a n) -> p a n", a=2)
            if kind < 2:
                w = (w_gate, w_up)[kind].rearrange("(c p) n -> p c n", p=P)
                src = w[:, 2 * half:2 * half + 2, SQ * j:SQ * j + SQ]
            else:
                src = w_down[SQ * j:SQ * j + SQ, :].rearrange("(p m) d -> p m d", m=M)[:, 2 * half:2 * half + 2, :]
            sp.dma_start(dst, src).then_inc(w_loaded[q % 3], 16)

        with ExitStack() as ctx:
            def sb(name, shape, dt=F32):
                return ctx.enter_context(nc.sbuf_tensor(name, shape, dt))

            def pb(name, shape, dt=F32):
                return ctx.enter_context(nc.psum_tensor(name, shape, dt))

            kv_sb = sb("kv_sb", [P, 2, KT, P])
            v_ones = sb("v_ones", [P, 2, KT, HG, VW + 1])
            kT_hi = sb("kT_hi", [P, SKP], F32R)
            kT_lo = sb("kT_lo", [P, SKP], F32R)
            qT_hi = sb("qT_hi", [P, SQ], F32R)
            qT_lo = sb("qT_lo", [P, SQ], F32R)
            k_stack = sb("k_stack", [3 * HD + 1, 4 * 2, SKP], F32R)
            q_stack = sb("q_stack", [3 * HD + 1, 4 * 2, SQ], F32R)
            xq = sb("xq", [P, 2, QT, P])
            probs = sb("probs", [P, P_RING, SQ])
            oT = sb("oT", [64 + VW, 2, SQ])
            ident_b = sb("ident_b", [P, P], BF16)
            hidden = sb("hidden", [P, 512])
            hidden_out = sb("hidden_out", [P, 512])
            shift_u = sb("shift_u", [P, UNITS, QT])
            rstd_u = sb("rstd_u", [P, UNITS, QT])
            max_part = sb("max_part", [P, 2, 2, NCH])
            neg_max = sb("neg_max", [P, 2, 2, QT], BF16)
            den_inv = sb("den_inv", [P, QT, 2])
            att = sb("att", [P, QT, 2, HD])
            amax_part = sb("amax_part", [P, 3, 8, 1])
            amax = sb("amax", [P, 3])
            amax_all = sb("amax_all", [P, 3])
            pow2 = sb("pow2", [P, 3])

            ps_max = [pb(f"ps_max{i}", [P, 512]) for i in range(M_BANKS)]
            ps_s = [pb(f"ps_s{i}", [P, 512]) for i in range(S_BANKS)]
            ps_o = pb("ps_o", [P, 512])
            ps_t = pb("ps_t", [P, 512])
            ps_m = pb("ps_m", [P, 512])

            consts_zero = sem("consts_zero")
            consts_ready = sem("consts_ready")
            ones_row = sem("ones_row")
            kv_loaded = [sem("kv_loaded0"), sem("kv_loaded1")]
            v_ready = sem("v_ready")
            unit_stats = sem("unit_stats")
            xq_ready = sem("xq_ready")
            t_ready = sem("t_ready")
            hi_ready = sem("hi_ready")
            lo_ready = sem("lo_ready")
            stack_loaded = [sem(f"stack_loaded{i}") for i in range(4)]
            scan_loaded = sem("scan_loaded")
            scan_read = sem("scan_read")
            amax_ready = sem("amax_ready")
            amax_shared = sem("amax_shared")
            scale_chain = sem("scale_chain")
            max_scored = sem("max_scored")
            max_read = sem("max_read")
            neg_ready = sem("neg_ready")
            row_ready = sem("row_ready")
            row_copied = sem("row_copied")
            s_ready = sem("s_ready")
            masked = sem("masked")
            exp_done = sem("exp_done")
            pv_done = sem("pv_done")
            o_copied = sem("o_copied")
            ot_ready = sem("ot_ready")
            tail_chain = sem("tail_chain")
            x_added = sem("x_added")

            block = ctx.enter_context(nc.Block())

            LOOPS = UNITS // 2 - 1

            def all_periods(eng, period):
                period(0, 0, True, 2)
                with eng.Fori(0, LOOPS) as it:
                    for c in range(1, 4):
                        period(it, c, True, 2)
                    period(it + 1, 0, True, 2)
                for c in range(1, 4):
                    period(LOOPS, c, False, 3 - c)

            NORM_STEPS = [4, 6, 7, 9]

            SCAN_STEPS = [6, 8, 10]

            def is_first(p):
                return isinstance(p, int) and p == 0

            CHUNKS_IN = [[3, 3, 2, 2, 2, 3, 2, 2, 2, 2, 1, 1, 1], [3, 3, 2, 2, 2, 3, 3, 2, 1, 2, 1, 1, 1],
                         [3, 3, 2, 2, 2, 3, 2, 2, 2, 2, 1, 1, 1], [3, 3, 2, 2, 1, 3, 2, 2, 2, 2, 1, 2, 1]]
            PLACES = {0: (), 1: (0,), 2: (1, 2), 3: (1, 2, 2), 4: (0, 0, 2, 2)}

            def chunks_at(p, c, kt, left):
                if is_first(p):
                    chunks = range(3 * kt, 3 * kt + 3)
                    return [(1 + i // (2 * NCH), 1 + i // (2 * NCH), i % (2 * NCH)) for i in chunks]
                done = sum(CHUNKS_IN[c][:kt])
                return [(p + 1, (c + 1) % 4, NCH + i) if i < NCH else (p + 2, (c + 2) % 4, i - NCH)
                        for i in range(done, done + CHUNKS_IN[c][kt]) if left > i // NCH]

            def score_bank(kt, hh, left):
                return ps_s[hh] if left or kt % 2 == 1 else ps_max[hh]

            START_BANKS = [ps_t, ps_m, ps_s[0], ps_s[1], ps_t]
            START_CHUNKS = {14: 0, 17: 1, 20: 2, 22: 3, 24: 4}

            def turn_bank(v, i):
                return START_BANKS[i] if isinstance(v, int) and v < 2 else ps_t

            def max_reads_before(p, i):
                n = 2 * NCH
                last = i - M_BANKS if i >= M_BANKS else (n - 1 - (n - 1 - i) % M_BANKS) - n
                return n * p + last + 1 + M_BANKS

            TURN_STEPS = {0: {8: 0, 10: 1, 12: 2}, 1: {1: 3, 3: 4}}

            def join_step(p):
                return 9 if is_first(p) else 7

            def row_steps(p):
                return (10, 11) if is_first(p) else (9, 10)

            @block.sync
            def _(sp):
                for i, g in enumerate((g_xattn, g_ffn)):
                    sp.dma_start(gates[:, i:i + 1], g.rearrange("(a n) -> a n", a=1).partition_broadcast(P)
                                 ).then_inc(gates_loaded, 16)

                def load_kv(b, g, par):
                    src = ctx_v[b, g]
                    sp.dma_start(kv_sb[:, par, 0:KT - 1, :],
                                 src[0:(KT - 1) * P, :].rearrange("(t p) d -> p t d", p=P)
                                 ).then_inc(kv_loaded[par], 16)
                    sp.dma_start(kv_sb[0:KLAST, par, KT - 1, :], src[(KT - 1) * P:SK, :]
                                 ).then_inc(kv_loaded[par], 16)

                def load_x(b):
                    for g in range(G):
                        sp.dma_start(x_sb[:, b * G + g, :, :], x_v[:, b, g]).then_inc(x_loaded[min(b, 1)], 16)

                def scan_weights(n):
                    sp.wait_ge(scan_read, 3 * n + 3)
                    sp.sem_inc(sp_passed, 1)
                    for i, w in enumerate((w_gate, w_up, w_down)):
                        src = w.rearrange("a n -> (a n)").rearrange("(p n k) -> n p k", p=P, k=SCAN)
                        sp.dma_start(w_raw[:, i, :], src[n]).then_inc(scan_loaded, 16)

                def fill_stacks(v, par, r):
                    if not (isinstance(v, int) and v < 2):
                        sp.wait_ge(s_ready, EXPS * (2 * (v - 2) + r + 1))
                    for done, stack, parts in ((TG - 1, k_stack, (kT_hi, kT_hi, kT_lo)),
                                               (TG, q_stack, (qT_hi, qT_lo, qT_hi))):
                        sp.wait_ge(lo_ready, TG * v + done)
                        for j in (2 * r, 2 * r + 1):
                            for n, part in enumerate(parts):
                                sp.dma_start(stack[HD * n:HD * n + HD, 4 * par + j, :].bitcast(F32),
                                             part[HD * j:HD * j + HD, :].bitcast(F32)
                                             ).then_inc(stack_loaded[2 * par + r], 16)

                def free_kv(v):
                    sp.wait_ge(t_ready, TG * v + GROUPS)
                    sp.sem_inc(sp_passed, 1)
                    sp.wait_ge(v_ready, 2 * (v + 1))
                    sp.sem_inc(sp_passed, 1)

                load_x(0)
                load_kv(0, 0, 0)
                load_kv(0, 1, 1)
                fill_stacks(0, 0, 0)
                fill_stacks(0, 0, 1)
                for b in range(1, B):
                    load_x(b)
                free_kv(0)
                load_kv(0, 2, 0)
                fill_stacks(1, 1, 0)

                def period(it, c, more, left):
                    par, r = c // 2, c % 2
                    u = 2 * it + par
                    if r == 0 and (more or c == 0):
                        fill_stacks(u + 1, 1 - par, 1)
                    if c == 1:
                        scan_weights(it)
                    if r == 1 and more:
                        free_kv(u + 1)
                        if c == 1:
                            load_kv((it + 1) // 2, 2 * ((it + 1) % 2) + 1, 1)
                        else:
                            load_kv(((it + 2) // 2) % B, 2 * ((it + 2) % 2), 0)
                        fill_stacks(u + 2, par, 0)

                all_periods(sp, period)
                sp.wait_ge(scan_read, 24 + 3)
                for q in range(3):
                    load_piece(sp, q)
                sp.wait_ge(kv_loaded[0], 32 * (UNITS // 2 + 1))

            @block.gpsimd
            def _(pool):
                pool.memset(ident[:, :], 0.0)
                pool.memset(ident_b[:, :], 0.0)
                pool.memset(kT_hi[:, SK:SKP].bitcast(F32), 0.0)
                pool.memset(kT_lo[:, SK:SKP].bitcast(F32), 0.0)
                pool.memset(hidden[:, :], 0.0).then_inc(consts_zero, 1)
                pool.wait_ge(consts_zero, 1)
                for m in (ident, ident_b):
                    pool.affine_select(out=m[:, :], in_=m[:, :], compare_op=ALU.not_equal, fill=1.0,
                                       base=0, pattern=[[-1, P]], channel_multiplier=1)
                pool.affine_select(out=hidden[:, 512 - P:], in_=hidden[:, 512 - P:], compare_op=ALU.is_gt, fill=MASKED,
                                   base=0, pattern=[[-1, P]], channel_multiplier=1).then_inc(consts_ready, 1)

                pool.memset(v_ones[:, :, :, :, :], 1.0)
                pool.memset(oT[:, :, :], 0.0).then_inc(consts_zero, 1)

                def copy_v(v, loads, par):
                    pool.wait_ge(kv_loaded[par], 32 * loads)
                    if not (isinstance(v, int) and v < 2):
                        pool.wait_ge(pv_done, 2 * EXPS * (v - 1) + P_RING)
                    pool.sem_inc(pool_passed, 1)
                    pool.tensor_copy(v_ones[:, par, 0:KT - 1, :, 0:HD],
                                     kv_sb[:, par, 0:KT - 1, :].rearrange("p t (h d) -> p t h d", h=HG)
                                     ).then_inc(v_ready, 1)
                    pool.tensor_copy(v_ones[0:KLAST, par, KT - 1, :, 0:HD],
                                     kv_sb[0:KLAST, par, KT - 1, :].rearrange("p (h d) -> p h d", h=HG)
                                     ).then_inc(v_ready, 1)

                pool.wait_ge(consts_zero, 2)
                copy_v(0, 1, 0)

                def clear_hidden(p, c, kt, hh):
                    e, (c0, w) = 2 * kt + hh, diagonal(kt)
                    pool.wait_ge(exp_done, EXPS * p + e + 1 + S_BANKS)
                    pool.sem_inc(pool_passed, 1)
                    tile = probs[0:key_rows(kt), (EXPS * c + e) % P_RING, 0:w]
                    pool.affine_select(out=tile, in_=tile, compare_op=ALU.is_gt, fill=0.0, base=c0,
                                       pattern=[[1, w]], channel_multiplier=-1).then_inc(masked, 1)

                def period(it, c, more, left):
                    par = c // 2
                    if c == 0 or (c == 2 and more):
                        copy_v(2 * it + par + 1, it + 1 + par, 1 - par)
                    if c == 3 and not more:
                        pool.wait_ge(amax_ready, 1)
                        pool.partition_all_reduce(amax_all[:, :], amax[:, :], P, bass.bass_isa.ReduceOp.max
                                                  ).then_inc(amax_shared, 1)
                    for kt in range(KT):
                        for hh in range(2):
                            if diagonal(kt):
                                clear_hidden(4 * it + c, c, kt, hh)

                all_periods(pool, period)

            @block.scalar
            def _(act):
                act.sem_inc(exp_done, S_BANKS)
                act.sem_inc(o_copied, 1)
                act.wait_ge(gates_loaded, 32)
                act.activation(tanhs[:, :], gates[:, :], ACT.Tanh).then_inc(tanh_ready, 1)

                def round_hi(v, i):
                    act.wait_ge(t_ready, TG * v + i + 1)
                    if i < GROUPS:
                        w = min(512, SK - 512 * i)
                        act.activation(kT_hi[:, 512 * i:512 * i + w], turn_bank(v, i)[:, 0:w], ACT.Copy
                                       ).then_inc(hi_ready, 1)
                    else:
                        act.activation(qT_hi[:, :], turn_bank(v, i)[:, :], ACT.Copy).then_inc(hi_ready, 1)

                def norm_q(v, par, tiles):
                    for t in tiles:
                        last = act.activation(xq[:, par, t, :], x_sb[:, v, t, :], ACT.Identity,
                                              bias=shift_u[:, v, t:t + 1], scale=rstd_u[:, v, t:t + 1])
                    if QT - 1 in tiles:
                        last.then_inc(xq_ready, 1)

                def copy_row(p, c, hh):
                    act.wait_ge(row_ready, 2 * p + hh + 1)
                    act.activation(q_stack[3 * HD:3 * HD + 1, 2 * c + hh, :], ps_m[3 * HD:3 * HD + 1, :],
                                   ACT.Copy).then_inc(row_copied, 1)

                def copy_o(p, c):
                    act.wait_ge(pv_done, EXPS * (p + 1) + P_RING)
                    act.wait_ge(ot_ready, p + 1)
                    act.activation(oT[:, c % 2, :], ps_o[0:64 + VW, :], ACT.Copy).then_inc(o_copied, 1)

                for i in range(GROUPS):
                    round_hi(0, i)
                act.wait_ge(unit_stats, 2)
                norm_q(0, 0, range(QT))
                round_hi(0, GROUPS)
                norm_q(1, 1, range(QT))
                act.wait_ge(consts_zero, 2)
                act.activation(k_stack[3 * HD:3 * HD + 1, :, :],
                               v_ones[3 * HD:3 * HD + 1, 0, 0, 0, HD:HD + 1].unsqueeze(1).to_broadcast([1, 8, SKP]),
                               ACT.Copy).then_inc(ones_row, 1)
                for i in (0, 1):
                    act.wait_ge(stack_loaded[i], 16 * STACK_DMAS)
                for i in range(TG):
                    round_hi(1, i)
                for hh in range(2):
                    copy_row(0, 0, hh)

                def period(it, c, more, left):
                    p = 4 * it + c
                    u = 2 * it + c // 2
                    for kt in range(KT):
                        K, w = key_rows(kt), SQ - q_start(kt)
                        for hh in range(2):
                            e = 2 * kt + hh
                            act.wait_ge(s_ready, EXPS * p + e + 1)
                            act.wait_ge(pv_done, EXPS * p + e + 1)
                            act.activation(probs[0:K, (EXPS * c + e) % P_RING, 0:w], score_bank(kt, hh, left)[0:K, 0:w],
                                           ACT.Exp, scale=SCALE).then_inc(exp_done, 1)
                        if kt == 0 and not is_first(p):
                            copy_o(p - 1, (c + 3) % 4)
                        if more and kt in TURN_STEPS[c % 2]:
                            if TURN_STEPS[c % 2][kt] == 0:
                                for r in range(2):
                                    act.wait_ge(stack_loaded[2 * (1 - c // 2) + r],
                                                16 * STACK_DMAS * (it + 1 + c // 2))
                            round_hi(u + 2, TURN_STEPS[c % 2][kt])
                        if c % 2 == 0 and more and kt in NORM_STEPS:
                            if kt == NORM_STEPS[0]:
                                act.wait_ge(unit_stats, 2 if is_first(p) else 2 * ((it + 1) // 2 + 1))
                                act.sem_inc(act_passed, 1)
                            norm_q((u + 2) % UNITS, c // 2, (NORM_STEPS.index(kt),))
                        if left and kt in row_steps(p):
                            copy_row(p + 1, (c + 1) % 4, row_steps(p).index(kt))

                all_periods(act, period)
                copy_o(4 * LOOPS + 3, 3)

            @block.vector
            def _(dve):
                dve.sem_inc(max_read, M_BANKS)
                dve.sem_inc(scan_read, 3)
                dve.memset(ps_o[:, :], 0.0)

                def unit_norms(turn, b):
                    dve.wait_ge(rstd_ready, turn + 1)
                    to = [w[:, :, :].rearrange("p (b g) t -> p b g t", b=B)[:, b] for w in (rstd_u, shift_u)]
                    over = [w[:, b, :].unsqueeze(1).to_broadcast([P, G, QT]) for w in (rstd, mean)]
                    dve.tensor_copy(to[0], over[0]).then_inc(unit_stats, 1)
                    dve.scalar_tensor_tensor(to[1], over[1], -1.0, over[0], ALU.mult, ALU.mult
                                             ).then_inc(unit_stats, 1)

                def rest_lo(v, i):
                    dve.wait_ge(hi_ready, TG * v + i + 1)
                    if i < GROUPS:
                        s = slice(512 * i, min(SK, 512 * i + 512))
                        dve.tensor_tensor(kT_lo[:, s], turn_bank(v, i)[:, 0:s.stop - s.start], kT_hi[:, s].bitcast(F32),
                                          ALU.subtract).then_inc(lo_ready, 1)
                    else:
                        dve.tensor_tensor(qT_lo[:, :], turn_bank(v, i)[:, :], qT_hi[:, :].bitcast(F32),
                                          ALU.subtract).then_inc(lo_ready, 1)

                def read_max(p, c, i):
                    hh, n = i // NCH, i % NCH
                    dve.wait_ge(max_scored, 2 * NCH * p + i + 1)
                    (t, _, w), bank, part = CHUNKS[n], ps_max[i % M_BANKS], max_part[:, c % 2, hh, n:n + 1]
                    if n + 1 < NCH and CHUNKS[n + 1][0] == t:
                        dve.tensor_reduce(part, bank[:, 0:w], AX.X, ALU.max).then_inc(max_read, 1)
                    else:
                        dve.sem_inc(dve_passed, 1)
                        dve.tensor_tensor_reduce(hidden_out[:, 0:w], bank[:, 0:w], hidden[:, 512 - w:], 1.0, -3e38,
                                                 ALU.add, ALU.max, part).then_inc(max_read, 1)

                def join_max(p, c):
                    dve.wait_ge(max_read, 2 * NCH * (p + 1) + M_BANKS)
                    n, t = PER_T[0], PER_T.index(PER_T[-1])
                    dve.tensor_reduce(neg_max[:, c % 2, :, 0:t],
                                      max_part[:, c % 2, :, 0:n * t].rearrange("p h (t n) -> p h t n", n=n),
                                      AX.X, ALU.max, negate=True).then_inc(neg_ready, 1)
                    dve.tensor_reduce(neg_max[:, c % 2, :, t:QT],
                                      max_part[:, c % 2, :, n * t:NCH].rearrange("p h (t n) -> p h t n", t=QT - t),
                                      AX.X, ALU.max, negate=True).then_inc(neg_ready, 1)

                def add_attention(p, c, u, part):
                    o = ps_m[:, :].rearrange("p (t w) -> p t w", t=QT)[:, :, 0:2 * 64].rearrange(
                        "p t (h w) -> p t h w", h=2)
                    if part == 0:
                        dve.wait_ge(ot_ready, p + 3)
                        dve.reciprocal(den_inv[:, :, :], o[:, :, :, HD]).then_inc(tail_chain, 1)
                    elif part == 1:
                        dve.wait_ge(tail_chain, 2 * p + 1)
                        dve.tensor_tensor(att[:, :, :, :], o[:, :, :, 0:HD],
                                          den_inv[:, :, :].unsqueeze(3).to_broadcast([P, QT, 2, HD]), ALU.mult
                                          ).then_inc(tail_chain, 1)
                    else:
                        dve.wait_ge(tail_chain, 2 * p + 2)
                        xs = x_sb[:, u, :, 64 * (c % 2):64 * (c % 2) + 64]
                        dve.scalar_tensor_tensor(xs, att[:, :, :, :].rearrange("p t h d -> p t (h d)"),
                                                 tanhs[:, 0:1], xs, ALU.mult, ALU.add).then_inc(x_added, 1)

                dve.wait_ge(x_loaded[0], 16 * G)
                for i in range(NORM_PARTS):
                    norm_part(dve, 0, 0, i)
                    if QT - 1 <= i < QT - 1 + GROUPS:
                        rest_lo(0, i - (QT - 1))
                unit_norms(0, 0)
                rest_lo(0, GROUPS)
                for i in range(2 * NCH):
                    read_max(0, 0, i)
                    if i in START_CHUNKS:
                        rest_lo(1, START_CHUNKS[i])
                join_max(0, 0)
                dve.wait_ge(tanh_ready, 1)

                def read_scan(n, i):
                    dve.wait_ge(scan_loaded, 48 * (n + 1))
                    dve.tensor_reduce(amax_part[:, i, n, :], w_raw[:, i, :], AX.X, ALU.max,
                                      apply_absolute_value=True).then_inc(scan_read, 1)

                def join_scans():
                    dve.wait_ge(scan_read, 24 + 3)
                    dve.tensor_reduce(amax[:, :], amax_part[:, :, :, 0], AX.X, ALU.max).then_inc(amax_ready, 1)

                def weight_scales():
                    dve.wait_ge(amax_shared, 1)
                    dve.tensor_scalar(amax[:, :], amax_all[:, :], 1e-30, None, ALU.max).then_inc(scale_chain, 1)
                    dve.wait_ge(scale_chain, 1)
                    dve.tensor_scalar(pow2[:, :].bitcast(U32), amax[:, :].bitcast(U32), 0x7F800000, None,
                                      ALU.bitwise_and).then_inc(scale_chain, 1)
                    dve.wait_ge(scale_chain, 2)
                    dve.tensor_scalar(inv_scale[:, :], pow2[:, :], 2.0 ** -14, None, ALU.mult
                                      ).then_inc(scale_chain, 1)
                    dve.wait_ge(scale_chain, 3)
                    dve.reciprocal(w_scale[:, :], inv_scale[:, :]).then_inc(scale_chain, 1)

                def period(it, c, more, left):
                    p = 4 * it + c
                    u = 2 * it + c // 2
                    more_stats = more and c >= 2
                    if c == 2 and not more:
                        join_scans()
                    for kt in range(KT):
                        if left and kt == join_step(p):
                            join_max(p + 1, (c + 1) % 4)
                        prev = 2 * it - 1 if c == 0 else 2 * it + (c - 1) // 2
                        parts = [] if is_first(p) else {2: [0], 3: [1, 2]}.get(kt, [])
                        for n, chunk in enumerate(chunks_at(p, c, kt, left)):
                            read_max(*chunk)
                            if n < len(parts):
                                add_attention(p - 1, (c + 3) % 4, prev, parts[n])
                        for part in parts[len(chunks_at(p, c, kt, left)):]:
                            add_attention(p - 1, (c + 3) % 4, prev, part)
                        if more and kt in TURN_STEPS[c % 2]:
                            rest_lo(u + 2, TURN_STEPS[c % 2][kt])
                        if c == 1 and kt in SCAN_STEPS:
                            read_scan(it, SCAN_STEPS.index(kt))
                        if c == 3 and not more and kt == 5:
                            weight_scales()
                            for i in range(NORM_PARTS):
                                norm_part(dve, LOOPS + 1, B - 2, i)
                            norm_tokens(dve, 0, range(QT))
                        part = kt - 3 if c == 2 and kt < 3 + QT else kt - 5 + QT if c == 3 and kt >= 5 else -1
                        if more_stats and 0 <= part < NORM_PARTS:
                            if part == 0:
                                dve.wait_ge(x_loaded[1], 16 * G * (B - 1))
                                dve.wait_ge(x_added, p)
                                dve.sem_inc(dve_passed, 1)
                            norm_part(dve, it + 1, (it + 1) % B, part)
                        if more_stats and part == NORM_PARTS:
                            unit_norms(it + 1, (it + 1) % B)

                all_periods(dve, period)
                for part in range(3):
                    add_attention(4 * LOOPS + 3, 3, 2 * LOOPS + 1, part)

            @block.tensor
            def _(pe):
                pe.sem_inc(pv_done, P_RING)
                pe.sem_inc(ot_ready, 2)
                pe.wait_ge(consts_ready, 1)

                def turn(v, loads, par, i):
                    bank = turn_bank(v, i)
                    if not (isinstance(v, int) and v < 2):
                        pe.wait_ge(lo_ready, TG * v + i)
                    elif i == TG - 1 or v == 1:
                        pe.wait_ge(lo_ready, TG * v + 1 if i == TG - 1 else TG)
                    if i < GROUPS:
                        pe.wait_ge(kv_loaded[par], 32 * loads)
                        for t in range(4 * i, min(KT, 4 * i + 4)):
                            K = key_rows(t)
                            last = pe.transpose(bank[:, P * (t % 4):P * (t % 4) + K], kv_sb[0:K, par, t, :],
                                                ident[0:K, 0:K])
                    else:
                        pe.wait_ge(xq_ready, v + 1)
                        for t in range(QT):
                            last = pe.transpose(bank[:, P * t:P * t + P], xq[:, par, t, :], ident[:, :])
                    last.then_inc(t_ready, 1)

                def score_max(p, c, i, base=0, ahead=0):
                    hh, n = i // NCH, i % NCH
                    t, a, w = CHUNKS[n]
                    bank = ps_max[i % M_BANKS]
                    pe.wait_ge(max_read, base + max_reads_before(ahead, i))
                    pe.matmul(bank[:, 0:w], q_stack[0:3 * HD, 2 * c + hh, P * t:P * t + P],
                              k_stack[0:3 * HD, 2 * c + hh, a:a + w], start=True, stop=True).then_inc(max_scored, 1)

                def max_row(p, c, hh):
                    pe.wait_ge(neg_ready, 2 * (p + 1))
                    for t in range(QT):
                        last = pe.matmul(ps_m[3 * HD:3 * HD + 1, P * t:P * t + P], neg_max[:, c % 2, hh, t:t + 1],
                                         ident_b[:, :], start=True, stop=True)
                    last.then_inc(row_ready, 1)

                def score(p, c, kt, hh, left):
                    K, q0, slot = key_rows(kt), q_start(kt), 2 * c + hh
                    bank = score_bank(kt, hh, left)
                    e = 2 * kt + hh
                    pe.wait_ge(exp_done, EXPS * p + e + (1 if left else -1))
                    if not left and e == 0:
                        pe.wait_ge(max_read, 8 * NCH * (LOOPS + 1) + M_BANKS)
                    pe.matmul(bank[0:K, 0:SQ - q0], k_stack[:, slot, P * kt:P * kt + K],
                              q_stack[:, slot, q0:SQ], start=True, stop=True).then_inc(s_ready, 1)

                def values(p, c, kt, hh, unit=None):
                    K, q0, e = key_rows(kt), q_start(kt), 2 * kt + hh
                    if diagonal(kt):
                        pe.wait_ge(masked, MASKED_TILES * p + e - (EXPS - MASKED_TILES) + 1)
                    else:
                        pe.wait_ge(exp_done, EXPS * p + e + 1 + S_BANKS)
                    if kt == 0 and hh == 0:
                        pe.wait_ge(o_copied, p + 1)
                        pe.wait_ge(v_ready, 2 * unit + 2)
                    pe.matmul(ps_o[64 * hh:64 * hh + VW, q0:SQ],
                              v_ones[0:K, c // 2, kt, 2 * (c % 2) + hh, 0:VW],
                              probs[0:K, (EXPS * c + e) % P_RING, 0:SQ - q0],
                              start=kt == 0, stop=kt == KT - 1, skip_group_check=True).then_inc(pv_done, 1)

                def turn_o(p, c):
                    pe.wait_ge(o_copied, p + 2)
                    for t in range(QT):
                        last = pe.transpose(ps_m[:, P * t:P * t + 64 + VW], oT[:, c % 2, P * t:P * t + P],
                                            ident[0:64 + VW, 0:64 + VW])
                    last.then_inc(ot_ready, 1)

                for i in range(TG):
                    turn(0, 1, 0, i)
                pe.wait_ge(stack_loaded[0], 16 * STACK_DMAS)
                for i in range(2 * NCH):
                    score_max(0, 0, i)
                    if i in START_CHUNKS:
                        turn(1, 1, 1, START_CHUNKS[i])
                pe.wait_ge(ones_row, 1)
                pe.wait_ge(lo_ready, 2 * TG)
                max_row(0, 0, 0)
                pe.wait_ge(row_copied, 1)
                max_row(0, 0, 1)

                def period(it, c, more, left):
                    p = 4 * it + c
                    u = 2 * it + c // 2
                    first = is_first(p)
                    base = 2 * NCH * p
                    for kt in range(KT):
                        chunks = chunks_at(p, c, kt, left)

                        def maxima(place):
                            for n, chunk in enumerate(chunks):
                                if PLACES[len(chunks)][n] == place:
                                    if first and chunk[2] == 0:
                                        pe.wait_ge(stack_loaded[chunk[1]], 16 * STACK_DMAS)
                                    elif chunk[2] == 0:
                                        pe.wait_ge(stack_loaded[(c + 2) % 4], 16 * STACK_DMAS * (it + 1 + c // 2))
                                    score_max(*chunk, base, 2 if chunk[1] == (c + 2) % 4 else 1)

                        if kt == 0:
                            pe.wait_ge(row_copied, 2 * (p + 1))
                        score(p, c, kt, 0, left)
                        maxima(0)
                        score(p, c, kt, 1, left)
                        maxima(1)
                        if more and kt in TURN_STEPS[c % 2]:
                            turn(u + 2, it + 2, c // 2, TURN_STEPS[c % 2][kt])
                        if kt == 2 and not first:
                            turn_o(p - 1, (c + 3) % 4)
                        if left and kt == row_steps(p)[0]:
                            if not first:
                                pe.wait_ge(x_added, p)
                            max_row(p + 1, (c + 1) % 4, 0)
                        if left and kt == row_steps(p)[1]:
                            pe.wait_ge(row_copied, 2 * (p + 1) + 1)
                            max_row(p + 1, (c + 1) % 4, 1)
                        for hh in range(2):
                            if kt > 0:
                                values(p, c, kt - 1, hh, u)
                            elif not first:
                                values(p - 1, (c + 3) % 4, KT - 1, hh)
                        maxima(2)

                all_periods(pe, period)
                p = 4 * LOOPS + 3
                for hh in range(2):
                    values(p, 3, KT - 1, hh)
                pe.wait_ge(x_added, p)
                turn_o(p, 3)

        with ExitStack() as ctx:
            def sb(name, shape, dt=F32):
                return ctx.enter_context(nc.sbuf_tensor(name, shape, dt))

            def pb(name, shape, dt=F32):
                return ctx.enter_context(nc.psum_tensor(name, shape, dt))

            IT = JB * M
            X_SCALE = 256.0
            HID_SCALE = 2.0 ** -50

            wg_hi, wg_lo, wu_hi, wu_lo = (sb(n, [P, JB, M, G, P], F16) for n in ("wg_hi", "wg_lo", "wu_hi", "wu_lo"))
            wd_hi, wd_lo = (sb(n, [P, JB, M, D], F16) for n in ("wd_hi", "wd_lo"))
            xT_hi = sb("xT_hi", [P, G, SQ], F16)
            xT_lo = sb("xT_lo", [P, G, SQ], F16)
            silu = sb("silu", [P, 2, SQ])
            hid = sb("hid", [P, 2, SQ])
            mag = sb("mag", [P, M, SQ])
            hid_hi = sb("hid_hi", [P, M, SQ], F16)
            hid_lo = sb("hid_lo", [P, M, SQ], F16)
            beats = sb("beats", [P, 6, SQ], F16)
            wins = sb("wins", [P, M, SQ], F16)
            kept_hi = sb("kept_hi", [P, M, SQ], F16)
            kept_lo = sb("kept_lo", [P, M, SQ], F16)
            tanh_scale = sb("tanh_scale", [P, 1])
            out_scale = sb("out_scale", [P, 1])

            ps_g = [pb(f"ps_g{i}", [P, 512]) for i in range(2)]
            ps_u = [pb(f"ps_u{i}", [P, 512]) for i in range(2)]
            ps_d = [pb(f"ps_d{i}", [P, 512]) for i in range(QT)]

            w_round = sem("w_round")
            w_scaled = sem("w_scaled")
            factors = sem("factors")
            xt_turned = sem("xt_turned")
            xt_hi_ready = sem("xt_hi_ready")
            xt_lo_ready = sem("xt_lo_ready")
            gate_ready = sem("gate_ready")
            up_ready = sem("up_ready")
            tanh_done = sem("tanh_done")
            silu_ready = sem("silu_ready")
            hid_ready = sem("hid_ready")
            mag_ready = sem("mag_ready")
            hid_hi_ready = sem("hid_hi_ready")
            hid_lo_ready = sem("hid_lo_ready")
            beats_ready = sem("beats_ready")
            wins_ready = sem("wins_ready")
            kept_ready = sem("kept_ready")
            down_ready = sem("down_ready")
            kept_used = sem("kept_used")
            y_ready = sem("y_ready")
            y_stored = sem("y_stored")

            block = ctx.enter_context(nc.Block())

            def weights_of(q):
                j, kind, half = *ORDER[q // 2], q % 2
                if kind < 2:
                    hi, lo = ((wg_hi, wg_lo), (wu_hi, wu_lo))[kind]
                    return kind, *(w[:, j, :, 2 * half:2 * half + 2, :].rearrange("p m c n -> p m (c n)")
                                   for w in (hi, lo))
                return kind, *(w[:, j, 2 * half:2 * half + 2, :] for w in (wd_hi, wd_lo))

            def raw(q):
                if ORDER[q // 2][1] < 2:
                    return w_raw[:, q % 3, :].rearrange("p (n m) -> p m n", m=M)
                return w_raw[:, q % 3, :].rearrange("p (a n) -> p a n", a=2)

            def pieces_after(i):
                j, m = i // M, i % M
                q = 4 + 6 * j + 2 * m
                return range(q, q + 2) if m < 3 and 4 <= q < PIECES else ()

            def all_batches(eng, batch):
                batch(0)
                with eng.Fori(1, B - 1) as b:
                    batch(b)
                batch(B - 1)

            def is_batch(b, n):
                return isinstance(b, int) and b == n

            XT_BANKS = [ps_g[0], ps_u[0], ps_g[1], ps_u[1]]

            @block.sync
            def _(sp):
                for q in range(3, PIECES):
                    load_piece(sp, q)

                def store(b):
                    for t in range(QT):
                        sp.wait_ge(y_ready, QT * b + t + 1)
                        sp.sem_inc(sp_passed, 1)
                        xv = x_sb[:, :, t, :].rearrange("p (b g) d -> p b g d", b=B)
                        sp.dma_start(out_v[b, t].rearrange("p (g d) -> p g d", g=G), xv[:, b]).then_inc(y_stored, 16)

                with sp.Fori(0, B) as b:
                    store(b)
                sp.wait_ge(y_stored, 16 * B * QT)

            @block.gpsimd
            def _(pool):
                for n, q in enumerate(q for q in range(PIECES) if ORDER[q // 2][1] == 2):
                    kind, hi, lo = weights_of(q)
                    pool.wait_ge(w_round, q + 1)
                    pool.tensor_scalar(raw(q), raw(q), w_scale[:, kind:kind + 1], None, ALU.mult
                                       ).then_inc(w_scaled, 1)
                    pool.wait_ge(w_scaled, n + 1)
                    pool.tensor_tensor(lo, raw(q), hi, ALU.subtract).then_inc(wd_rest, 1)

            @block.scalar
            def _(act):
                def split(q):
                    kind, hi, _lo = weights_of(q)
                    act.wait_ge(w_loaded[q % 3], 16 * (q // 3 + 1))
                    act.activation(hi, raw(q), ACT.Copy, scale=w_scale[:, kind:kind + 1]).then_inc(w_round, 1)

                def turned_hi(b):
                    for c in range(G):
                        act.wait_ge(xt_turned, G * b + c + 1)
                        if c == 0 and not is_batch(b, 0):
                            act.wait_ge(up_ready, IT * b)
                        act.activation(xT_hi[:, c, :], XT_BANKS[c][:, :], ACT.Copy, scale=X_SCALE
                                       ).then_inc(xt_hi_ready, 1)

                def batch(b):
                    first = is_batch(b, 0)
                    if first:
                        split(0)
                        turned_hi(0)
                        for q in (1, 2, 3):
                            split(q)
                        act.wait_ge(factors, 2)
                    for i in range(IT):
                        n = IT * b + i
                        s = i % 2
                        act.wait_ge(gate_ready, n + 1)
                        if not (first and i < 2):
                            act.wait_ge(hid_ready, n - 1)
                        act.activation(silu[:, s, :], ps_g[s][:, :], ACT.Tanh, scale=tanh_scale[:, 0:1]
                                       ).then_inc(tanh_done, 1)
                        act.wait_ge(hid_ready, n + 1)
                        if i % M == 0 and not (first and i == 0):
                            act.wait_ge(kept_ready, JB * b + i // M)
                        act.activation(mag[:, i % M, :], hid[:, s, :], ACT.Abs).then_inc(mag_ready, 1)
                        act.activation(hid_hi[:, i % M, :], hid[:, s, :], ACT.Copy).then_inc(hid_hi_ready, 1)
                        if first:
                            for q in pieces_after(i):
                                split(q)
                    if not is_batch(b, B - 1):
                        turned_hi(b + 1)

                all_batches(act, batch)

            @block.vector
            def _(dve):
                def turned_lo(b):
                    for c in range(G):
                        dve.wait_ge(xt_hi_ready, G * b + c + 1)
                        dve.scalar_tensor_tensor(xT_lo[:, c, :], XT_BANKS[c][:, :], X_SCALE, xT_hi[:, c, :],
                                                 ALU.mult, ALU.subtract).then_inc(xt_lo_ready, 1)

                def split_rest(q):
                    kind, hi, lo = weights_of(q)
                    dve.wait_ge(w_round, q + 1)
                    dve.scalar_tensor_tensor(lo, raw(q), w_scale[:, kind:kind + 1], hi, ALU.mult, ALU.subtract
                                             ).then_inc(w_rest, 1)

                def compare(k):
                    dve.wait_ge(mag_ready, M * (k + 1))
                    dve.tensor_tensor(beats[:, 0:3, :], mag[:, 0:3, :], mag[:, 1:4, :], ALU.is_ge)
                    dve.tensor_tensor(beats[:, 3:5, :], mag[:, 0:2, :], mag[:, 2:4, :], ALU.is_ge)
                    dve.tensor_tensor(beats[:, 5, :], mag[:, 0, :], mag[:, 3, :], ALU.is_ge
                                      ).then_inc(beats_ready, 1)
                    dve.wait_ge(beats_ready, k + 1)
                    dve.tensor_tensor(wins[:, 0:2, :], beats[:, 0:2, :], beats[:, 3:5, :], ALU.add)
                    dve.tensor_tensor(wins[:, 2, :], beats[:, 2, :], beats[:, 3, :], ALU.subtract)
                    dve.tensor_tensor(wins[:, 3, :], beats[:, 2, :], beats[:, 4, :], ALU.add
                                      ).then_inc(wins_ready, 1)
                    dve.wait_ge(wins_ready, 3 * k + 1)
                    dve.tensor_tensor(wins[:, 1:3, :], wins[:, 1:3, :], beats[:, 0:2, :], ALU.subtract)
                    dve.tensor_tensor(wins[:, 0, :], wins[:, 0, :], beats[:, 5, :], ALU.add)
                    dve.tensor_tensor(wins[:, 3, :], wins[:, 3, :], beats[:, 5, :], ALU.add
                                      ).then_inc(wins_ready, 1)

                def select(k):
                    dve.wait_ge(wins_ready, 3 * k + 2)
                    for m, (least, op) in enumerate(((1.5, ALU.is_gt), (0.5, ALU.is_gt), (-0.5, ALU.is_gt),
                                                     (1.5, ALU.is_lt))):
                        last = dve.tensor_scalar(wins[:, m, :], wins[:, m, :], least, None, op)
                    last.then_inc(wins_ready, 1)
                    dve.wait_ge(wins_ready, 3 * k + 3)
                    dve.wait_ge(hid_lo_ready, M * (k + 1))
                    if not (isinstance(k, int) and k == 0):
                        dve.wait_ge(kept_used, k)
                    dve.tensor_tensor(kept_hi[:, :, :], hid_hi[:, :, :], wins[:, :, :], ALU.mult)
                    dve.tensor_tensor(kept_lo[:, :, :], hid_lo[:, :, :], wins[:, :, :], ALU.mult
                                      ).then_inc(kept_ready, 1)

                def add_down(b, tiles):
                    for t in tiles:
                        dve.wait_ge(down_ready, QT * b + t + 1)
                        xv = x_sb[:, :, t, :].rearrange("p (b g) d -> p b g d", b=B)[:, b]
                        dve.scalar_tensor_tensor(xv, ps_d[t][:, :].rearrange("p (g d) -> p g d", g=G),
                                                 out_scale[:, 0:1], xv, ALU.mult, ALU.add).then_inc(y_ready, 1)

                def batch(b):
                    first = is_batch(b, 0)
                    if first:
                        split_rest(0)
                        turned_lo(0)
                        for q in (1, 2, 3):
                            split_rest(q)
                    for i in range(IT):
                        n = IT * b + i
                        s = i % 2
                        dve.wait_ge(tanh_done, n + 1)
                        dve.scalar_tensor_tensor(silu[:, s, :], silu[:, s, :], 1.0, ps_g[s][:, :],
                                                 ALU.add, ALU.mult).then_inc(silu_ready, 1)
                        dve.wait_ge(silu_ready, n + 1)
                        dve.wait_ge(up_ready, n + 1)
                        if not (first and i < 2):
                            dve.wait_ge(hid_lo_ready, n - 1)
                        dve.scalar_tensor_tensor(hid[:, s, :], silu[:, s, :], HID_SCALE, ps_u[s][:, :],
                                                 ALU.mult, ALU.mult).then_inc(hid_ready, 1)
                        if i % M == 0 and not (first and i == 0):
                            select(JB * b + i // M - 1)
                        dve.wait_ge(hid_hi_ready, n + 1)
                        dve.tensor_tensor(hid_lo[:, i % M, :], hid[:, s, :], hid_hi[:, i % M, :],
                                          ALU.subtract).then_inc(hid_lo_ready, 1)
                        if first:
                            for q in pieces_after(i):
                                if ORDER[q // 2][1] < 2:
                                    split_rest(q)
                        if first and i == STATS_TILE:
                            for part in range(NORM_PARTS):
                                norm_part(dve, LOOPS + 2, B - 1, part)
                        if not first and i in ADD_TILES:
                            add_down(b - 1, ADD_TILES[i])
                        if not is_batch(b, B - 1) and i in NORM_TILES:
                            if i == min(NORM_TILES):
                                dve.wait_ge(xt_turned, G * (b + 1))
                            norm_tokens(dve, b + 1, NORM_TILES[i])
                        if i == IT - 1 and not is_batch(b, B - 1):
                            turned_lo(b + 1)
                        if i % M == M - 1:
                            compare(JB * b + i // M)

                STATS_TILE = 10
                ADD_TILES = {4: (0, 1), 5: (2,), 6: (3,)}
                NORM_TILES = {12: (0, 1), 13: (2, 3)}
                dve.tensor_scalar(tanh_scale[:, :], inv_scale[:, 0:1], 0.5 / X_SCALE, None, ALU.mult
                                  ).then_inc(factors, 1)
                dve.tensor_scalar(out_scale[:, :], inv_scale[:, 0:1], inv_scale[:, 1:2],
                                  0.5 / (X_SCALE * X_SCALE * HID_SCALE), ALU.mult, ALU.mult).then_inc(factors, 1)
                dve.wait_ge(factors, 2)
                dve.tensor_scalar(out_scale[:, :], out_scale[:, :], inv_scale[:, 2:3], tanhs[:, 1:2],
                                  ALU.mult, ALU.mult).then_inc(factors, 1)
                dve.wait_ge(factors, 3)
                all_batches(dve, batch)
                select(JB * B - 1)
                add_down(B - 1, range(QT))

            @block.tensor
            def _(pe):
                def down(b, j, behind=None):
                    k = JB * b + j
                    pe.wait_ge(kept_ready, k + 1)
                    if j == 0 and not is_batch(b, 0):
                        pe.wait_ge(y_ready, QT * b)
                    for t in range(QT):
                        if t == 2 and behind:
                            behind()
                        rows = slice(P * t, P * t + P)
                        for m in range(M):
                            for n, (a, w) in enumerate(((kept_hi, wd_hi), (kept_hi, wd_lo), (kept_lo, wd_hi))):
                                last = pe.matmul(ps_d[t][:, :], a[:, m, rows], w[:, j, m, :],
                                                 start=(j == 0 and m == 0 and n == 0),
                                                 stop=(j == JB - 1 and m == M - 1 and n == 2))
                        if j == JB - 1:
                            last.then_inc(down_ready, 1)
                        elif t == QT - 1:
                            last.then_inc(kept_used, 1)
                    if j == JB - 1:
                        pe.sem_inc(kept_used, 1)

                def turn_x(b):
                    pe.wait_ge(xn_ready, QT * (b + 1))
                    for c in range(G):
                        if not is_batch(b, 0):
                            pe.wait_ge(hid_ready if c % 2 else silu_ready, IT * b - 1 + c // 2)
                        for t in range(QT):
                            last = pe.transpose(XT_BANKS[c][:, P * t:P * t + P], xn[:, t, c, :], ident[:, :])
                        last.then_inc(xt_turned, 1)

                def batch(b):
                    first = is_batch(b, 0)
                    if first:
                        turn_x(0)
                    pe.wait_ge(xt_lo_ready, G * (b + 1))
                    for i in range(IT):
                        j, m = i // M, i % M
                        n = IT * b + i
                        s = i % 2
                        if first and m == 0:
                            wait_split(pe, 2 * ORDER.index((j, 0)) + 1)
                        for w_hi, w_lo, bank, read, ready in ((wg_hi, wg_lo, ps_g[s], silu_ready, gate_ready),
                                                              (wu_hi, wu_lo, ps_u[s], hid_ready, up_ready)):
                            if not (first and i < 2):
                                pe.wait_ge(read, n - 1)
                            if first and m == 0 and bank is ps_u[0]:
                                wait_split(pe, 2 * ORDER.index((j, 1)) + 1)
                            for c in range(G):
                                for k, (w, xx) in enumerate(((w_hi, xT_hi), (w_hi, xT_lo), (w_lo, xT_hi))):
                                    last = pe.matmul(bank[:, :], w[:, j, m, c, :], xx[:, c, :],
                                                     start=c == 0 and k == 0, stop=c == G - 1 and k == 2)
                            last.then_inc(ready, 1)
                        if i == M - 1 and not first:
                            wait_split(pe, PIECES - 1)
                            down(b - 1, JB - 1)
                        if m == M - 1 and j > 0:
                            if first:
                                wait_split(pe, 2 * ORDER.index((j - 1, 2)) + 1)
                            last_block = j == JB - 1 and not is_batch(b, B - 1)
                            down(b, j - 1, (lambda: turn_x(b + 1)) if last_block else None)

                all_batches(pe, batch)
                down(B - 1, JB - 1)


_INS = ["x", "ctx_2048", "g_xattn", "g_ffn", "L0_ffn_w_gate", "L0_ffn_w_up", "L0_ffn_w_down"]


def kernel(**inputs):
    import numpy as _np
    import concourse.bacc as _bacc
    from concourse import mybir as _mybir
    from concourse.bass_utils import run_bass_kernel_spmd as _run

    nc = _bacc.Bacc("TRN2", target_bir_lowering=False, num_devices=1)
    arrays, args = {}, []
    for name in _INS:
        a = _np.ascontiguousarray(inputs[name])
        arrays[f"in_{name}_dram"] = a
        args.append(nc.dram_tensor(f"in_{name}_dram", a.shape, _mybir.dt.from_np(a.dtype), kind="ExternalInput").ap())
    shape = _np.asarray(inputs["x"]).shape
    y = nc.dram_tensor("out_0_dram", shape, _mybir.dt.float32, kind="ExternalOutput").ap()
    gated_cross_attention_ffn(nc, *args, y)
    r = _run(nc, [arrays], core_ids=[0])
    return r.results[0]["out_0_dram"]
```
